# Optimizing a Trainium2 kernel written in Bass

```python
import numpy as np
import jax
import jax.numpy as jnp

def _softmax(x, axis=-1):
    return jax.nn.softmax(x, axis=axis)

def _gelu(x):
    return jax.nn.gelu(x, approximate=True)

def _silu(x):
    return jax.nn.silu(x)

def _sigmoid(x):
    return jax.nn.sigmoid(x)

def _layernorm(x, axis=-1, eps=1e-05):
    m = jnp.mean(x, axis=axis, keepdims=True)
    v = jnp.var(x, axis=axis, keepdims=True)
    return (x - m) / jnp.sqrt(v + eps)

def _scatter_add(tgt, idx, src, axis=0):
    return tgt.at[idx].add(src)

def _segment_sum(src, seg, n):
    return jax.ops.segment_sum(src, seg, n)
kernel_name = 'mk_xattn_seq_d2_seqx_r4_300357'

def setup_inputs(seed: int=0):
    np.random.seed(seed)
    _w = jnp.asarray

    def _rec_inputs():
        import jax
        import jax.numpy as jnp
        _rk = jax.random.key(seed)
        x = -0.000125 + 0.9999 * jax.random.normal(jax.random.fold_in(_rk, 1), (16, 256, 512), jnp.float32)
        _lenS = 256 - jax.random.randint(jax.random.fold_in(_rk, 7), (16,), 0, max(1, 256 // 4) + 1, jnp.int32)
        _lenS2 = 256 - jax.random.randint(jax.random.fold_in(_rk, 8), (16,), 0, max(1, 256 // 4) + 1, jnp.int32)
        _ctx_2048P = jax.random.normal(jax.random.fold_in(_rk, 11), (16, 16, 512), jnp.float32)
        _ctx_2048c = jax.random.dirichlet(jax.random.fold_in(_rk, 511), 0.3 * jnp.ones((16,), jnp.float32), (16, 256))
        _ctx_2048t = jnp.einsum('bsk,bkd->bsd', _ctx_2048c, _ctx_2048P)
        _ctx_2048t = _ctx_2048t * jax.lax.rsqrt(jnp.mean(jnp.square(_ctx_2048t)) + 1e-12) * 0.953939
        ctx_2048 = -1.52775e-05 + 0.999936 * (_ctx_2048t + 0.3 * jax.random.normal(jax.random.fold_in(_rk, 611), (16, 256, 512), jnp.float32))
        _validS = jnp.arange(256)[None, :] < _lenS[:, None]
        _validS2 = jnp.arange(256)[None, :] < _lenS2[:, None]
        _causal = jnp.tril(jnp.ones((256, 256), dtype=bool))
        mask_BxS2_bf1 = jnp.ones((16, 256), dtype=bool)
        return (x, ctx_2048, mask_BxS2_bf1)
    x, ctx_2048, mask_BxS2_bf1 = _rec_inputs()

    def _L0_xattn_setup():
        import jax, jax.numpy as jnp
        import numpy as np
        B, C, CI, N = (16, 256, 128, 512)
        EPS = 1e-05

        def _conv1x1(w, b, x):
            return jnp.einsum('oc,bcn->bon', w, x) + b[None, :, None]
        key = jax.random.key(seed)
        ks = jax.random.split(key, 14)
        s = 0.02
        return {'x': jax.random.normal(ks[0], (B, C, N), jnp.float32), 'x_2': jax.random.normal(ks[1], (B, C, N), jnp.float32), 'theta_w': jax.random.normal(ks[2], (CI, C), jnp.float32) * s, 'theta_b': jax.random.normal(ks[3], (CI,), jnp.float32) * s, 'phi_w': jax.random.normal(ks[4], (CI, C), jnp.float32) * s, 'phi_b': jax.random.normal(ks[5], (CI,), jnp.float32) * s, 'g_w': jax.random.normal(ks[6], (CI, C), jnp.float32) * s, 'g_b': jax.random.normal(ks[7], (CI,), jnp.float32) * s, 'w_w': jax.random.normal(ks[8], (C, CI), jnp.float32) * s, 'w_b': jax.random.normal(ks[9], (C,), jnp.float32) * s, 'bn_gamma': jax.random.normal(ks[10], (C,), jnp.float32), 'bn_beta': jax.random.normal(ks[11], (C,), jnp.float32), 'bn_mean': jax.random.normal(ks[12], (C,), jnp.float32), 'bn_var': jax.random.uniform(ks[13], (C,), jnp.float32, 0.5, 1.5)}
    _L0_xattn_all = _L0_xattn_setup()
    _L0_xattn_in = {k: v for k, v in _L0_xattn_all.items() if k in ('theta_w', 'theta_b', 'phi_w', 'phi_b', 'g_w', 'g_b', 'w_w', 'w_b', 'bn_gamma', 'bn_beta', 'bn_mean', 'bn_var')}
    del _L0_xattn_all

    def _L1_xattn_setup():
        import jax, jax.numpy as jnp
        import numpy as np
        HIDDEN = 512
        HEADS = 16
        HEAD_DIM = HIDDEN // HEADS
        LN_EPS = 1e-05
        GATE_INIT = 0.5

        def _layer_norm(x, gamma, beta):
            mu = jnp.mean(x, axis=-1, keepdims=True)
            var = jnp.mean(jnp.square(x - mu), axis=-1, keepdims=True)
            return (x - mu) * jax.lax.rsqrt(var + LN_EPS) * gamma + beta
        key = jax.random.key(seed)
        ks = jax.random.split(key, 8)
        B, T_TEXT, T_AUDIO = (4, 512, 375)
        s = 0.02
        return {'hidden_states': jax.random.normal(ks[0], (B, T_TEXT, HIDDEN), jnp.float32), 'audio_kv': jax.random.normal(ks[1], (B, T_AUDIO, HIDDEN), jnp.float32), 'audio_attention_mask': jnp.ones((B, T_AUDIO), dtype=bool), 'Wq': jax.random.normal(ks[2], (HIDDEN, HIDDEN), jnp.float32) * s, 'Wk': jax.random.normal(ks[3], (HIDDEN, HIDDEN), jnp.float32) * s, 'Wv': jax.random.normal(ks[4], (HIDDEN, HIDDEN), jnp.float32) * s, 'Wo': jax.random.normal(ks[5], (HIDDEN, HIDDEN), jnp.float32) * s, 'ln_gamma': jnp.ones((HIDDEN,), jnp.float32), 'ln_beta': jnp.zeros((HIDDEN,), jnp.float32), 'gate': jnp.array([GATE_INIT], jnp.float32)}
    _L1_xattn_all = _L1_xattn_setup()
    _L1_xattn_in = {k: v for k, v in _L1_xattn_all.items() if k in ('Wq', 'Wk', 'Wv', 'Wo', 'ln_gamma', 'ln_beta', 'gate')}
    del _L1_xattn_all
    return {'x': x, 'ctx_2048': ctx_2048, 'mask_BxS2_bf1': mask_BxS2_bf1, 'L0_xattn_theta_w': _L0_xattn_in['theta_w'], 'L0_xattn_theta_b': _L0_xattn_in['theta_b'], 'L0_xattn_phi_w': _L0_xattn_in['phi_w'], 'L0_xattn_phi_b': _L0_xattn_in['phi_b'], 'L0_xattn_g_w': _L0_xattn_in['g_w'], 'L0_xattn_g_b': _L0_xattn_in['g_b'], 'L0_xattn_w_w': _L0_xattn_in['w_w'], 'L0_xattn_w_b': _L0_xattn_in['w_b'], 'L0_xattn_bn_gamma': _L0_xattn_in['bn_gamma'], 'L0_xattn_bn_beta': _L0_xattn_in['bn_beta'], 'L0_xattn_bn_mean': _L0_xattn_in['bn_mean'], 'L0_xattn_bn_var': _L0_xattn_in['bn_var'], 'L1_xattn_Wq': _L1_xattn_in['Wq'], 'L1_xattn_Wk': _L1_xattn_in['Wk'], 'L1_xattn_Wv': _L1_xattn_in['Wv'], 'L1_xattn_Wo': _L1_xattn_in['Wo'], 'L1_xattn_ln_gamma': _L1_xattn_in['ln_gamma'], 'L1_xattn_ln_beta': _L1_xattn_in['ln_beta'], 'L1_xattn_gate': _L1_xattn_in['gate']}

def reference(x, ctx_2048, mask_BxS2_bf1, L0_xattn_theta_w, L0_xattn_theta_b, L0_xattn_phi_w, L0_xattn_phi_b, L0_xattn_g_w, L0_xattn_g_b, L0_xattn_w_w, L0_xattn_w_b, L0_xattn_bn_gamma, L0_xattn_bn_beta, L0_xattn_bn_mean, L0_xattn_bn_var, L1_xattn_Wq, L1_xattn_Wk, L1_xattn_Wv, L1_xattn_Wo, L1_xattn_ln_gamma, L1_xattn_ln_beta, L1_xattn_gate):
    import jax
    import jax.numpy as jnp

    def _L0_xattn_ref(x, x_2, theta_w, theta_b, phi_w, phi_b, g_w, g_b, w_w, w_b, bn_gamma, bn_beta, bn_mean, bn_var):
        import jax, jax.numpy as jnp
        import numpy as np
        B, C, CI, N = (16, 256, 128, 512)
        EPS = 1e-05

        def _conv1x1(w, b, x):
            return jnp.einsum('oc,bcn->bon', w, x) + b[None, :, None]
        g_x = _conv1x1(g_w, g_b, x_2).transpose(0, 2, 1)
        theta_x = _conv1x1(theta_w, theta_b, x).transpose(0, 2, 1)
        phi_x = _conv1x1(phi_w, phi_b, x_2)
        W = jnp.einsum('bnc,bcm->bnm', theta_x, phi_x) / phi_x.shape[-1]
        y = jnp.einsum('bnm,bmc->bnc', W, g_x).transpose(0, 2, 1)
        wy = _conv1x1(w_w, w_b, y)
        inv_std = jax.lax.rsqrt(bn_var + EPS)
        wy = bn_gamma[None, :, None] * (wy - bn_mean[None, :, None]) * inv_std[None, :, None] + bn_beta[None, :, None]
        return wy + x

    def _L1_xattn_ref(hidden_states, audio_kv, audio_attention_mask, Wq, Wk, Wv, Wo, ln_gamma, ln_beta, gate):
        import jax, jax.numpy as jnp
        import numpy as np
        HIDDEN = 512
        HEADS = 16
        HEAD_DIM = HIDDEN // HEADS
        LN_EPS = 1e-05
        GATE_INIT = 0.5

        def _layer_norm(x, gamma, beta):
            mu = jnp.mean(x, axis=-1, keepdims=True)
            var = jnp.mean(jnp.square(x - mu), axis=-1, keepdims=True)
            return (x - mu) * jax.lax.rsqrt(var + LN_EPS) * gamma + beta
        B, Tt, D = hidden_states.shape
        Ta = audio_kv.shape[1]
        scale = HEAD_DIM ** (-0.5)
        a = _layer_norm(audio_kv, ln_gamma, ln_beta)
        Q = (hidden_states @ Wq.T).reshape(B, Tt, HEADS, HEAD_DIM).transpose(0, 2, 1, 3)
        K = (a @ Wk.T).reshape(B, Ta, HEADS, HEAD_DIM).transpose(0, 2, 1, 3)
        V = (a @ Wv.T).reshape(B, Ta, HEADS, HEAD_DIM).transpose(0, 2, 1, 3)
        scores = jnp.einsum('bhtd,bhsd->bhts', Q, K) * scale
        mask = audio_attention_mask[:, None, None, :]
        scores = jnp.where(mask, scores, jnp.float32(-jnp.inf))
        attn = jax.nn.softmax(scores, axis=-1)
        out = jnp.einsum('bhts,bhsd->bhtd', attn, V)
        out = out.transpose(0, 2, 1, 3).reshape(B, Tt, D)
        out = out @ Wo.T
        return hidden_states + jnp.tanh(gate) * out
    x = _L0_xattn_ref(x, ctx_2048, L0_xattn_theta_w, L0_xattn_theta_b, L0_xattn_phi_w, L0_xattn_phi_b, L0_xattn_g_w, L0_xattn_g_b, L0_xattn_w_w, L0_xattn_w_b, L0_xattn_bn_gamma, L0_xattn_bn_beta, L0_xattn_bn_mean, L0_xattn_bn_var)
    x = _L1_xattn_ref(x, ctx_2048, mask_BxS2_bf1, L1_xattn_Wq, L1_xattn_Wk, L1_xattn_Wv, L1_xattn_Wo, L1_xattn_ln_gamma, L1_xattn_ln_beta, L1_xattn_gate)
    return x

_drawn_inputs = setup_inputs


def setup_inputs(seed=0):
    import zlib

    import numpy as np

    out = dict(_drawn_inputs(seed))
    spreads = {'L1_xattn_ln_gamma': (1.0, 0.6), 'L1_xattn_ln_beta': (0.0, 2.0)}
    factors = {'L0_xattn_theta_w': 3.488,
     'L0_xattn_theta_b': 8.0,
     'L0_xattn_phi_w': 3.353,
     'L0_xattn_phi_b': 8.0,
     'L0_xattn_g_w': 3.545,
     'L0_xattn_g_b': 8.0,
     'L0_xattn_w_w': 3.28,
     'L0_xattn_w_b': 4.236,
     'L1_xattn_Wq': 8.0,
     'L1_xattn_Wk': 8.0}
    for name, (base, spread) in spreads.items():
        noise = np.random.default_rng([zlib.crc32(name.encode()), seed]).standard_normal(out[name].shape)
        drawn = base * np.exp(spread * noise) if base else spread * noise
        out[name] = jnp.asarray(drawn.astype(out[name].dtype))
    for name, factor in factors.items():
        out[name] = (out[name] * factor).astype(out[name].dtype)
    return out
```

```python
from contextlib import ExitStack

import concourse.bass as bass
from concourse import mybir

F32 = mybir.dt.float32
F32R = mybir.dt.float32r
U8 = mybir.dt.uint8
ALU = mybir.AluOpType
ACT = mybir.ActivationFunctionType
AX = mybir.AxisListType

P = 128
LN_EPS = 1e-5
BN_EPS = 1e-5


def two_layer_cross_attention(
    nc, x, ctx2, mask, wpgT, thT, ww, cols, pgb, wkT, wqT, wvT, woT, mask_bias, out,
):
    B, C, N = x.shape
    CI = thT.shape[1]
    H = 16
    DH = N // H
    KC = C // P
    KN = N // P
    G = H // 4
    RQ = 3 * DH
    R_MASK, R_M = RQ, RQ + 1
    R_ALL = RQ + 3
    SCALE = float(DH) ** -0.5
    assert C == 256 and N == 512 and CI == P and DH == 32

    V_THB, V_GAM, V_BET, V_MEAN, V_VAR, V_WB, V_LG, V_LB, V_GATE = 0, 1, 3, 5, 7, 9, 11, 15, 19
    NV = 20

    with ExitStack() as ctx:
        def sb(name, shape, dt=F32):
            return ctx.enter_context(nc.sbuf_tensor(name, shape, dt))

        def bank(name):
            return ctx.enter_context(nc.psum_tensor(name, [P, 512], F32))

        per = {}

        def sem(name, each_sample):
            s = ctx.enter_context(nc.semaphore(name))
            per[name] = each_sample
            return (s, name)

        def after(eng, s, sample, k):
            value = per[s[1]] * sample + k
            if isinstance(value, int) and value <= 0:
                return
            eng.wait_ge(s[0], value)

        def after_plain(eng, s, sample, k):
            if not isinstance(sample, int):
                eng.wait_ge(vec_in[0], 48)
            after(eng, s, sample, k)

        wpg = sb("wpg", [P, 2, KC, 2 * CI], F32R)
        thw = sb("thw", [P, 2, KC, CI], F32R)
        wwT = sb("wwT", [P, 2, C], F32R)
        wk = sb("wk", [P, 2, KN, N], F32R)
        wq = sb("wq", [P, 2, KN, N], F32R)
        wv = sb("wv", [P, 2, KN, N], F32R)
        wo = sb("wo", [P, 2, KN, N], F32R)
        vec = sb("vec", [P, NV])
        bias_pg = sb("bias_pg", [P, 2 * CI])
        ident = sb("ident", [P, P])
        ones = sb("ones", [P, DH])
        neg_half = sb("neg_half", [P, 2])
        bn_scale = sb("bn_scale", [P, KC])
        bn_shift = sb("bn_shift", [P, KC])
        bn_tmp = sb("bn_tmp", [P, KC])
        gate_t = sb("gate_t", [P, 1])
        mask8 = sb("mask8", [B, C], U8)
        mask_row = sb("mask_row", [B, C], F32R)

        xin = sb("xin", [P, KC, N])
        cin = sb("cin", [P, KC, N])
        xhat = sb("xhat", [P, KC, N])
        xs = sb("xs", [P, 2, KC * N], F32R)
        cs = sb("cs", [P, 2, KC * N], F32R)
        pg32 = sb("pg32", [P, KN, 2 * CI])
        gp = sb("gp", [P, 2 * KC * N], F32R)
        ks = sb("ks", [P, 2, G, C], F32R)
        m32 = sb("m32", [P, 2, P])
        ms = sb("ms", [P, 2, P], F32R)
        as_ = sb("as_", [P, 2, C], F32R)
        ths = sb("ths", [P, 2, N], F32R)
        x1 = sb("x1", [P, KC, N])
        res = sb("res", [P, KC, N])
        a32 = sb("a32", [P, KN, C])
        kst = sb("kst", [P, H, C], F32R)
        qst = sb("qst", [P, H, C], F32R)
        vt = sb("vt", [P, KC, N])
        pt = sb("pt", [P, 8, 2 * C])
        rec = sb("rec", [P, C])
        os_ = sb("os_", [P, 2, G, C], F32R)
        mx = sb("mx", [P, 2, H])
        mrow = sb("mrow", [H, 2, C], F32R)
        st6 = sb("st6", [P, KC, 6])
        mv = sb("mv", [P, KC, 2])
        ve, ve2, dsq, mean = (sb(n, [P, KC]) for n in ("ve", "ve2", "dsq", "mean"))
        var_eps = sb("var_eps", [P, KC])
        rstd = sb("rstd", [P, KC])

        o32 = xhat[:, :, :].rearrange("p k n -> p (k n)").rearrange("p (g t) -> p g t", g=G)
        x1T = xs[:, :, :].rearrange("p a (k t) -> p a k t", k=KN)
        aT = cs[:, :, :].rearrange("p a (k t) -> p a k t", k=KN)
        xk = xs[:, :, :].rearrange("p a (k n) -> p a k n", k=KC)
        ck = cs[:, :, :].rearrange("p a (k n) -> p a k n", k=KC)
        gpv = gp[:, :].rearrange("p (m w a c) -> p m w a c", m=KN, w=2, a=2)
        qs = gp[:, :].rearrange("p (a g t) -> p a g t", a=2, g=G)
        m_bank_t = lambda b_: b_[:, :].rearrange("p (a c) -> p a c", a=2)

        ST = [bank("ST0"), bank("ST1")]
        PV = bank("PV")
        CB = [bank("C0"), bank("C1")]
        DB = [bank("D0"), bank("D1")]
        EB = bank("E")

        vec_in = sem("vec_in", 0)
        stage_in = [sem(f"stage_in{i}", 0) for i in range(5)]
        const_done = sem("const_done", 0)
        stack_set = sem("stack_set", 0)
        ident_set = sem("ident_set", 0)
        setup_v = sem("setup_v", 0)
        setup_bn = sem("setup_bn", 0)
        setup_g = sem("setup_g", 0)
        gate_done = sem("gate_done", 0)
        w_high = sem("w_high", 0)
        w_low = sem("w_low", 0)
        small_high = sem("small_high", 0)
        small_low = sem("small_low", 0)
        ww_scaled = sem("ww_scaled", 0)
        wwT_full = sem("wwT_full", 0)
        wwT_done = sem("wwT_done", 0)
        bias_stored = sem("bias_stored", 0)

        x_in, c_in = sem("x_in", 16), sem("c_in", 16)
        half_in = [sem(f"half{i}_in", 24 * 16) for i in range(2)]
        maskrow_in, mrow_in, stored = sem("maskrow_in", 16), sem("mrow_in", 32), sem("stored", 16)

        pg_full, th_full, aT_full = sem("pg_full", 2), sem("th_full", 1), sem("aT_full", 2)
        M_full, A_full, wy_full, x1T_full = sem("M_full", 1), sem("A_full", 1), sem("wy_full", 2), sem("x1T_full", 2)
        K_full, Q_full, V_full = sem("K_full", 2), sem("Q_full", 2), sem("V_full", 2)
        pre_full, mT_full = sem("pre_full", H), sem("mT_full", 1)
        ST_full, PV_full, O_full = sem("ST_full", H), sem("PV_full", G), sem("O_full", 2)

        pg32_done, pgH_done, pgL_done = sem("pg32_done", 2), sem("pgH_done", 2), sem("pgL_done", 2)
        thH_done, thL_done = sem("thH_done", 1), sem("thL_done", 1)
        a32_done, aH_done, aL_done = sem("a32_done", 4), sem("aH_done", 2), sem("aL_done", 2)
        m32_done, MH_done, ML_done = sem("m32_done", 2), sem("MH_done", 1), sem("ML_done", 1)
        AH_done, AL_done = sem("AH_done", 1), sem("AL_done", 1)
        x1_done, x1TH_done, x1TL_done = sem("x1_done", 2), sem("x1TH_done", 2), sem("x1TL_done", 2)
        KH_done, KL_done = sem("KH_done", 2), sem("KL_done", 2)
        QH_done, QL_done = sem("QH_done", 2), sem("QL_done", 2)
        V_done = sem("V_done", 2)
        max_done, mH_done, mL_done = sem("max_done", H), sem("mH_done", 1), sem("mL_done", 1)
        exp_done, rec_done, o32_done = sem("exp_done", H), sem("rec_done", G), sem("o32_done", G)
        oH_done, oL_done, out_done = sem("oH_done", 2), sem("oL_done", 2), sem("out_done", 2)
        res_done = sem("res_done", 1)
        st6_done, mv_done, ve_done, rstd_done, xhat_done = (
            sem("st6_done", 2), sem("mv_done", 5), sem("ve_done", 1), sem("rstd_done", 1), sem("xhat_done", 2))
        mean_done = sem("mean_done", 1)
        xH_done, xL_done = sem("xH_done", 1), sem("xL_done", 1)
        cH_done, cL_done = sem("cH_done", 1), sem("cL_done", 1)

        small = pg32[:, :, :].rearrange("p a b -> p (a b)")
        s_wpg = small[:, 0:512].rearrange("p (k n) -> p k n", k=KC)
        s_th = small[:, 512:768].rearrange("p (k n) -> p k n", k=KC)
        s_ww = small[:, 768:1024].rearrange("p (k n) -> p k n", k=KC)
        stage = [pt[:, 4 * i:4 * i + 4, :] for i in range(2)]
        big = [(wk, wkT), (wq, wqT), (wv, wvT), (wo, woT)]

        STN = [8 * (k // 8) + 2 * (k % 4) + (k % 8) // 4 for k in range(H)]

        block = ctx.enter_context(nc.Block())

        @block.sync
        def _(sp):
            def load_c(s):
                after_plain(sp, xhat_done, s, 0)
                after_plain(sp, cH_done, s, 0)
                after_plain(sp, cL_done, s, 0)
                sp.dma_start(cin[:, :, :], ctx2[s].rearrange("(k p) n -> p k n", p=P)).then_inc(c_in[0], 16)

            def load_x(s):
                after_plain(sp, x1_done, s, 0)
                after_plain(sp, xL_done, s, 0)
                sp.dma_start(xin[:, :, :], x[s].rearrange("(k p) n -> p k n", p=P)).then_inc(x_in[0], 16)

            def stack(dst, high, low, parts, half):
                d = dst[:, :, :].rearrange("p (f j g) t -> p f j g t", f=2, j=4)
                for row, part in enumerate(parts):
                    src = (high, low)[part]
                    for j in range(4):
                        sp.dma_start(d[DH * row:DH * row + DH, half, j, :, :].bitcast(F32),
                                     src[DH * j:DH * j + DH, 2 * half:2 * half + 2, :].bitcast(F32)).then_inc(half_in[half][0], 16)

            def stack_k(s, half):
                if half == 0:
                    pass
                after_plain(sp, ST_full, s, 8 * half - 8)
                after_plain(sp, KH_done, s, half + 1)
                after_plain(sp, KL_done, s, half + 1)
                stack(kst, ks[:, 0, :, :], ks[:, 1, :, :], (0, 0, 1), half)

            def stack_q(s, half):
                after_plain(sp, QH_done, s, half + 1)
                after_plain(sp, QL_done, s, half + 1)
                stack(qst, qs[:, 0, :, :], qs[:, 1, :, :], (0, 1, 0), half)

            sp.dma_start(small[:, 0:512], wpgT.rearrange("(k p) n -> p k n", p=P)).then_inc(stage_in[4][0], 16)
            sp.dma_start(s_th, thT.rearrange("(k p) n -> p k n", p=P)).then_inc(stage_in[4][0], 16)
            sp.dma_start(s_ww, ww.rearrange("(k p) n -> p k n", p=P)).then_inc(stage_in[4][0], 16)
            load_c(0)
            load_x(0)
            sp.dma_start(vec[:, :], cols).then_inc(vec_in[0], 16)
            sp.dma_start(bias_pg[:, :], pgb).then_inc(vec_in[0], 16)
            sp.dma_start(mask8[:, :], mask).then_inc(vec_in[0], 16)
            for i in range(4):
                if i >= 2:
                    sp.wait_ge(w_high[0], i - 1)
                    sp.wait_ge(w_low[0], i - 1)
                sp.dma_start(stage[i % 2], big[i][1].rearrange("(k p) n -> p k n", p=P)).then_inc(stage_in[i][0], 16)
            sp.wait_ge(setup_v[0], 1)
            sp.dma_start(mask_bias, mask_row[:, :].bitcast(F32)).then_inc(bias_stored[0], 16)
            sp.wait_ge(bias_stored[0], 16)

            def turn(cb, nb, pb):
                if pb is not None:
                    load_c(pb)
                if nb is not None:
                    stack_k(nb, 0)
                    if pb is not None:
                        load_x(pb)
                    stack_q(nb, 0)
                    stack_k(nb, 1)
                    if isinstance(nb, int) and nb == 0:
                        sp.wait_ge(stack_set[0], 2)
                    sp.dma_start(kst[R_MASK:R_MASK + 1, :, :].bitcast(F32),
                                 mask_bias[nb].rearrange("(o n) -> o n", o=1).unsqueeze(1).to_broadcast([1, H, C])
                                 ).then_inc(maskrow_in[0], 16)
                    stack_q(nb, 1)
                    for a, s in enumerate((mH_done, mL_done)):
                        after_plain(sp, s, nb, 1)
                        sp.dma_start(qst[R_M + a:R_M + a + 1, :, :].bitcast(F32), mrow[:, a, :].bitcast(F32)).then_inc(mrow_in[0], 16)
                if cb is not None:
                    after_plain(sp, out_done, cb, 2)
                    sp.dma_start(out[cb].rearrange("(k p) n -> p k n", p=P), res[:, :, :]).then_inc(stored[0], 16)

            turn(None, 0, 1)
            turn(0, 1, 2)
            with sp.Fori(1, B - 2) as i:
                turn(i, i + 1, i + 2)
            turn(B - 2, B - 1, None)
            turn(B - 1, None, None)
            after_plain(sp, stored, B, 0)

        @block.gpsimd
        def _(pool):
            pool.memset(ident[:, :], 0.0).then_inc(ident_set[0], 1)
            pool.memset(ones[:, :], 1.0).then_inc(const_done[0], 1)
            pool.memset(neg_half[:, :], -0.5).then_inc(const_done[0], 1)
            pool.wait_ge(ident_set[0], 1)
            pool.affine_select(out=ident[:, :], in_=ident[:, :], compare_op=ALU.not_equal, fill=1.0,
                               base=0, pattern=[[-1, P]], channel_multiplier=1).then_inc(const_done[0], 1)

            def make_rstd(s):
                after(pool, ve_done, s, 1)
                pool.tensor_tensor(rstd[:, :], var_eps[:, :], neg_half[:, :], ALU.pow).then_inc(rstd_done[0], 1)

            def x_low(s):
                after(pool, xH_done, s, 1)
                pool.tensor_tensor(xs[:, 1, :], xin[:, :, :].rearrange("p k n -> p (k n)"),
                                   xs[:, 0, :].bitcast(F32), ALU.subtract).then_inc(xL_done[0], 1)

            def c_low(s):
                after(pool, cH_done, s, 1)
                pool.tensor_tensor(cs[:, 1, :], cin[:, :, :].rearrange("p k n -> p (k n)"),
                                   cs[:, 0, :].bitcast(F32), ALU.subtract).then_inc(cL_done[0], 1)

            pool.wait_ge(const_done[0], 3)
            make_rstd(0)
            pool.wait_ge(setup_bn[0], 1)
            pool.tensor_tensor(bn_tmp[:, :], bn_scale[:, :], neg_half[:, :], ALU.pow).then_inc(setup_g[0], 1)
            c_low(0)
            x_low(0)

            pool.wait_ge(xL_done[0], 1)
            pool.memset(kst[RQ:P, :, :].bitcast(F32), -1.0).then_inc(stack_set[0], 1)
            pool.wait_ge(stack_set[0], 1)
            pool.memset(qst[RQ:P, :, :].bitcast(F32), 1.0).then_inc(stack_set[0], 1)
            pool.wait_ge(stack_set[0], 2)

            for n in range(4):
                pool.wait_ge(w_high[0], n + 1)
                w = big[n][0]
                pool.tensor_tensor(w[:, 1, :, :], stage[n % 2], w[:, 0, :, :].bitcast(F32),
                                   ALU.subtract).then_inc(w_low[0], 1)

            def turn(cb, nb, pb):
                if nb is not None:
                    for i in range(2):
                        after(pool, pgH_done, nb, i + 1)
                        src = pg32[:, 2 * i:2 * i + 2, :].rearrange("p m (w c) -> p m w c", w=2)
                        pool.tensor_tensor(gpv[:, 2 * i:2 * i + 2, :, 1, :], src,
                                           gpv[:, 2 * i:2 * i + 2, :, 0, :].bitcast(F32),
                                           ALU.subtract).then_inc(pgL_done[0], 1)
                    for i in range(2):
                        after(pool, aH_done, nb, i + 1)
                        pool.tensor_tensor(aT[:, 1, 2 * i:2 * i + 2, :], a32[:, 2 * i:2 * i + 2, :],
                                           aT[:, 0, 2 * i:2 * i + 2, :].bitcast(F32),
                                           ALU.subtract).then_inc(aL_done[0], 1)
                if cb is not None:
                    for i in range(2):
                        after(pool, oH_done, cb, i + 1)
                        pool.tensor_tensor(os_[:, 1, 2 * i:2 * i + 2, :], o32[:, 2 * i:2 * i + 2, :],
                                           os_[:, 0, 2 * i:2 * i + 2, :].bitcast(F32),
                                           ALU.subtract).then_inc(oL_done[0], 1)
                if pb is not None:
                    make_rstd(pb)
                    x_low(pb)
                    c_low(pb)

            turn(None, 0, 1)
            turn(0, 1, 2)
            with pool.Fori(1, B - 2) as i:
                turn(i, i + 1, i + 2)
            turn(B - 2, B - 1, None)
            turn(B - 1, None, None)

        @block.scalar
        def _(act):
            def x_high(s):
                after(act, x_in, s, 16)
                after(act, Q_full, s, 0)
                act.activation(xs[:, 0, :], xin[:, :, :].rearrange("p k n -> p (k n)"), ACT.Copy).then_inc(xH_done[0], 1)

            def c_high(s):
                after(act, c_in, s, 16)
                after(act, V_full, s, 0)
                act.activation(cs[:, 0, :], cin[:, :, :].rearrange("p k n -> p (k n)"), ACT.Copy).then_inc(cH_done[0], 1)

            c_high(0)
            x_high(0)
            act.wait_ge(vec_in[0], 48)
            act.activation(gate_t[:, :], vec[:, V_GATE:V_GATE + 1], ACT.Tanh).then_inc(gate_done[0], 1)
            for n in range(4):
                act.wait_ge(stage_in[n][0], 16)
                act.activation(big[n][0][:, 0, :, :], stage[n % 2], ACT.Copy).then_inc(w_high[0], 1)

            def turn(cb, nb, pb):
                def exp(k):
                    if cb is None:
                        return
                    if k % 4 == 0:
                        after(act, PV_full, cb, max(k // 4 - 1, 0))
                    if k == 0 and isinstance(cb, int) is False:
                        act.wait_ge(w_low[0], 4)
                    after(act, ST_full, cb, k + 1)
                    act.activation(pt[:, k % 8, :], ST[k % 2][:, :], ACT.Exp, scale=SCALE).then_inc(exp_done[0], 1)

                if cb is not None:
                    after(act, stored, cb, 0)
                    after(act, x1_done, cb, 2)
                    act.activation(res[:, :, :], x1[:, :, :], ACT.Copy).then_inc(res_done[0], 1)
                if nb is not None:
                    after(act, th_full, nb, 1)
                    after(act, A_full, nb, 0)
                    act.activation(ths[:, 0, :], EB[:, :], ACT.Identity,
                                   bias=vec[:, V_THB:V_THB + 1]).then_inc(thH_done[0], 1)
                exp(0)
                if nb is not None:
                    after(act, aL_done, nb, 0)
                    for d in range(KN):
                        after(act, aT_full, nb, d // 2 + 1)
                        act.activation(a32[:, d, :], DB[d // 2][:, (d % 2) * C:(d % 2) * C + C], ACT.Identity,
                                       bias=vec[:, V_LB + d:V_LB + d + 1],
                                       scale=vec[:, V_LG + d:V_LG + d + 1]).then_inc(a32_done[0], 1)
                for k in range(1, 8):
                    exp(k)

                def high(full, bank_, dst, i, s, done, free, free_k):
                    after(act, free, s, free_k)
                    after(act, full, s, i + 1)
                    act.activation(dst, bank_[:, :].rearrange("p (a t) -> p a t", a=2), ACT.Copy).then_inc(done[0], 1)

                if nb is not None:
                    high(K_full, DB[0], ks[:, 0, 0:2, :], 0, nb, KH_done, pre_full, 0)
                exp(8)
                exp(9)
                exp(10)
                if nb is not None:
                    for i in range(2):
                        high(x1T_full, CB[i], x1T[:, 0, 2 * i:2 * i + 2, :], i, nb, x1TH_done, th_full, 1)
                    high(K_full, DB[1], ks[:, 0, 2:4, :], 1, nb, KH_done, pre_full, 0)
                for k in range(11, 15):
                    exp(k)
                if nb is not None:
                    high(Q_full, DB[0], qs[:, 0, 0:2, :], 0, nb, QH_done, M_full, 1)
                exp(15)
                if nb is not None:
                    high(Q_full, DB[1], qs[:, 0, 2:4, :], 1, nb, QH_done, M_full, 1)
                    for i in range(2):
                        if cb is not None:
                            after(act, PV_full, cb, 4)
                        after(act, V_full, nb, i + 1)
                        act.activation(vt[:, i, :], CB[i][:, :], ACT.Copy).then_inc(V_done[0], 1)
                if pb is not None:
                    x_high(pb)
                    c_high(pb)

            turn(None, 0, 1)
            turn(0, 1, 2)
            with act.Fori(1, B - 2) as i:
                turn(i, i + 1, i + 2)
            turn(B - 2, B - 1, None)
            turn(B - 1, None, None)

        @block.vector
        def _(dve):
            def stats(s):
                after(dve, c_in, s, 16)
                for k in range(KC):
                    dve.bn_stats(st6[:, k, :], cin[:, k, :]).then_inc(st6_done[0], 1)
                after(dve, st6_done, s, KC)
                dve.tensor_tensor(mv[:, :, 0], st6[:, :, 1], st6[:, :, 4], ALU.add).then_inc(mv_done[0], 1)
                dve.tensor_tensor(mv[:, :, 1], st6[:, :, 1], st6[:, :, 4], ALU.subtract).then_inc(mv_done[0], 1)
                dve.tensor_tensor(ve[:, :], st6[:, :, 2], st6[:, :, 5], ALU.add).then_inc(mv_done[0], 1)
                after(dve, mv_done, s, 3)
                dve.tensor_scalar(mean[:, :], mv[:, :, 0], 0.5, None, ALU.mult).then_inc(mean_done[0], 1)
                dve.tensor_scalar(ve2[:, :], ve[:, :], 1.0 / N, LN_EPS, ALU.mult, ALU.add).then_inc(mv_done[0], 1)
                dve.scalar_tensor_tensor(out=dsq[:, :], in0=mv[:, :, 1], scalar=0.25, in1=mv[:, :, 1],
                                         op0=ALU.mult, op1=ALU.mult).then_inc(mv_done[0], 1)
                after(dve, mv_done, s, 5)
                dve.tensor_tensor(var_eps[:, :], ve2[:, :], dsq[:, :], ALU.add).then_inc(ve_done[0], 1)

            def normalise(s, o_sample):
                after(dve, aT_full, s, 0)
                if o_sample is not None:
                    after(dve, oL_done, o_sample, 2)
                after(dve, rstd_done, s, 1)
                after(dve, mean_done, s, 1)
                for k in range(KC):
                    dve.tensor_scalar(xhat[:, k, :], cin[:, k, :], mean[:, k:k + 1], rstd[:, k:k + 1],
                                      ALU.subtract, ALU.mult).then_inc(xhat_done[0], 1)

            stats(0)
            dve.wait_ge(vec_in[0], 48)
            dve.tensor_scalar(bn_scale[:, :], vec[:, V_VAR:V_VAR + KC], BN_EPS, None, ALU.add).then_inc(setup_bn[0], 1)
            dve.wait_ge(stage_in[4][0], 48)
            dve.tensor_copy(wpg[:, 0, :, :], s_wpg).then_inc(small_high[0], 1)
            dve.tensor_copy(thw[:, 0, :, :], s_th).then_inc(small_high[0], 1)
            dve.wait_ge(small_high[0], 2)
            dve.tensor_tensor(wpg[:, 1, :, :], s_wpg, wpg[:, 0, :, :].bitcast(F32), ALU.subtract).then_inc(small_low[0], 1)
            dve.tensor_tensor(thw[:, 1, :, :], s_th, thw[:, 0, :, :].bitcast(F32), ALU.subtract).then_inc(small_low[0], 1)
            normalise(0, None)
            dve.wait_ge(setup_g[0], 1)
            dve.tensor_tensor(bn_scale[:, :], bn_tmp[:, :], vec[:, V_GAM:V_GAM + KC], ALU.mult).then_inc(setup_bn[0], 1)
            dve.tensor_tensor(bn_shift[:, :], vec[:, V_WB:V_WB + KC], vec[:, V_MEAN:V_MEAN + KC],
                              ALU.subtract).then_inc(setup_bn[0], 1)
            dve.wait_ge(setup_bn[0], 3)
            dve.tensor_tensor(bn_tmp[:, :], bn_shift[:, :], bn_scale[:, :], ALU.mult).then_inc(setup_bn[0], 1)
            for k in range(KC):
                dve.tensor_scalar(s_ww[:, k, :], s_ww[:, k, :], bn_scale[:, k:k + 1], None,
                                  ALU.mult).then_inc(ww_scaled[0], 1)
            dve.wait_ge(setup_bn[0], 4)
            dve.tensor_tensor(bn_shift[:, :], bn_tmp[:, :], vec[:, V_BET:V_BET + KC], ALU.add).then_inc(setup_bn[0], 1)
            dve.tensor_scalar(rec[0:B, :], mask8[:, :], 1.0, 3e38, ALU.subtract, ALU.mult).then_inc(setup_bn[0], 1)
            dve.wait_ge(setup_bn[0], 6)
            dve.tensor_scalar(mask_row[:, :], rec[0:B, :], 1e3, None, ALU.mult).then_inc(setup_v[0], 1)
            dve.wait_ge(wwT_full[0], 1)
            dve.tensor_copy(wwT[:, 0, :], EB[:, 0:C]).then_inc(wwT_done[0], 1)
            dve.wait_ge(wwT_done[0], 1)
            dve.tensor_tensor(wwT[:, 1, :], EB[:, 0:C], wwT[:, 0, :].bitcast(F32), ALU.subtract).then_inc(wwT_done[0], 1)
            dve.wait_ge(gate_done[0], 1)

            def turn(cb, nb, pb):
                def low(done_h, bank_, dst, hi, i, s, done):
                    after(dve, done_h, s, i + 1)
                    dve.tensor_tensor(dst, bank_[:, :].rearrange("p (a t) -> p a t", a=2), hi.bitcast(F32),
                                      ALU.subtract).then_inc(done[0], 1)

                def attended(g):
                    if cb is None:
                        return
                    if g == 0:
                        if nb is not None:
                            after(dve, aT_full, nb, 2)
                        after(dve, oL_done, cb, 0)
                    after(dve, PV_full, cb, g + 1)
                    dve.reciprocal(rec[:, :], PV[:, C:2 * C]).then_inc(rec_done[0], 1)
                    after(dve, rec_done, cb, g + 1)
                    dve.tensor_tensor(o32[:, g, :], PV[:, 0:C], rec[:, :], ALU.mult).then_inc(o32_done[0], 1)
                    if g % 2:
                        i = g // 2
                        after(dve, O_full, cb, 0)
                        after(dve, o32_done, cb, g + 1)
                        dve.tensor_copy(os_[:, 0, g - 1:g + 1, :], o32[:, g - 1:g + 1, :]).then_inc(oH_done[0], 1)

                if nb is not None:
                    after(dve, pgL_done, nb, 0)
                    for i in range(2):
                        after(dve, pg_full, nb, i + 1)
                        dve.tensor_tensor(pg32[:, 2 * i:2 * i + 2, :], CB[i][:, :].rearrange("p (m n) -> p m n", m=2),
                                          bias_pg[:, :].unsqueeze(1).to_broadcast([P, 2, 2 * CI]), ALU.add
                                          ).then_inc(pg32_done[0], 1)
                        after(dve, pg32_done, nb, i + 1)
                        dve.tensor_copy(gpv[:, 2 * i:2 * i + 2, :, 0, :],
                                        pg32[:, 2 * i:2 * i + 2, :].rearrange("p m (w c) -> p m w c", w=2)
                                        ).then_inc(pgH_done[0], 1)
                    after(dve, thH_done, nb, 1)
                    dve.scalar_tensor_tensor(out=ths[:, 1, :], in0=EB[:, :], scalar=vec[:, V_THB:V_THB + 1],
                                             in1=ths[:, 0, :].bitcast(F32), op0=ALU.add,
                                             op1=ALU.subtract).then_inc(thL_done[0], 1)
                    for i in range(2):
                        after(dve, a32_done, nb, 2 * i + 2)
                        after(dve, pg_full, nb, 2)
                        dve.tensor_copy(aT[:, 0, 2 * i:2 * i + 2, :], a32[:, 2 * i:2 * i + 2, :]).then_inc(aH_done[0], 1)
                    after(dve, M_full, nb, 1)
                    dve.tensor_scalar(m32[:, 0, :], EB[:, 0:P], 1.0 / N, None, ALU.mult).then_inc(m32_done[0], 1)
                    after(dve, m32_done, nb, 1)
                    dve.scalar_tensor_tensor(out=m32[:, 1, :], in0=EB[:, P:2 * P], scalar=1.0 / N, in1=m32[:, 0, :],
                                             op0=ALU.mult, op1=ALU.add).then_inc(m32_done[0], 1)
                    after(dve, m32_done, nb, 2)
                    dve.tensor_copy(ms[:, 0, :], m32[:, 1, :]).then_inc(MH_done[0], 1)
                    after(dve, MH_done, nb, 1)
                    dve.tensor_tensor(ms[:, 1, :], m32[:, 1, :], ms[:, 0, :].bitcast(F32),
                                      ALU.subtract).then_inc(ML_done[0], 1)
                    after(dve, A_full, nb, 1)
                    dve.tensor_copy(as_[:, 0, :], EB[:, 0:C]).then_inc(AH_done[0], 1)
                    after(dve, AH_done, nb, 1)
                    dve.tensor_tensor(as_[:, 1, :], EB[:, 0:C], as_[:, 0, :].bitcast(F32),
                                      ALU.subtract).then_inc(AL_done[0], 1)
                attended(0)
                if nb is not None:
                    low(KH_done, DB[0], ks[:, 1, 0:2, :], ks[:, 0, 0:2, :], 0, nb, KL_done)
                    if cb is not None:
                        after(dve, res_done, cb, 1)
                    for i in range(KC):
                        after(dve, wy_full, nb, i + 1)
                        dve.scalar_tensor_tensor(out=x1[:, i, :], in0=CB[i][:, :], scalar=bn_shift[:, i:i + 1],
                                                 in1=xin[:, i, :], op0=ALU.add, op1=ALU.add).then_inc(x1_done[0], 1)
                attended(1)
                if nb is not None:
                    for i in range(2):
                        low(x1TH_done, CB[i], x1T[:, 1, 2 * i:2 * i + 2, :], x1T[:, 0, 2 * i:2 * i + 2, :],
                            i, nb, x1TL_done)
                    low(KH_done, DB[1], ks[:, 1, 2:4, :], ks[:, 0, 2:4, :], 1, nb, KL_done)
                attended(2)
                if nb is not None:
                    for i in range(2):
                        low(QH_done, DB[i], qs[:, 1, 2 * i:2 * i + 2, :], qs[:, 0, 2 * i:2 * i + 2, :], i, nb, QL_done)
                attended(3)
                if pb is not None:
                    stats(pb)

                def final(i):
                    if cb is None:
                        return
                    after(dve, O_full, cb, i + 1)
                    after(dve, res_done, cb, 1)
                    dve.scalar_tensor_tensor(out=res[:, i, :], in0=CB[i][:, :], scalar=gate_t[:, 0:1],
                                             in1=res[:, i, :], op0=ALU.mult, op1=ALU.add).then_inc(out_done[0], 1)

                for n in range(H):
                    if nb is not None:
                        after(dve, pre_full, nb, n + 1)
                        dve.tensor_reduce(mx[:, :, n], DB[n % 2][:, :].rearrange("p (a s) -> p a s", a=2),
                                          AX.X, ALU.max).then_inc(max_done[0], 1)
                    if n == 2 and pb is not None:
                        normalise(pb, cb)
                    if n == 9:
                        final(0)
                if nb is not None:
                    after(dve, mT_full, nb, 1)
                    dve.tensor_copy(mrow[:, 0, :], EB[0:H, 0:C]).then_inc(mH_done[0], 1)
                    after(dve, mH_done, nb, 1)
                    dve.tensor_tensor(mrow[:, 1, :], EB[0:H, 0:C], mrow[:, 0, :].bitcast(F32),
                                      ALU.subtract).then_inc(mL_done[0], 1)
                final(1)

            turn(None, 0, 1)
            turn(0, 1, 2)
            with dve.Fori(1, B - 2) as i:
                turn(i, i + 1, i + 2)
            turn(B - 2, B - 1, None)
            turn(B - 1, None, None)

        @block.tensor
        def _(pe):
            pe.wait_ge(const_done[0], 3)
            pe.wait_ge(ww_scaled[0], 2)
            for k in range(KC):
                last = pe.transpose(EB[:, k * P:(k + 1) * P], s_ww[:, k, :], ident[:, :])
            last.then_inc(wwT_full[0], 1)
            pe.wait_ge(small_low[0], 2)

            PASSES = ((0, 0), (0, 1), (1, 0))

            def product(dst, depth, left, right, only=None):
                jobs = [(k, a, b) for k in range(depth) for a, b in PASSES]
                last = None
                for n, (k, a, b) in enumerate(jobs):
                    if only is None or n in only:
                        last = pe.matmul(dst, left(a, k), right(b, k), start=(n == 0), stop=(n == len(jobs) - 1))
                return last

            def turn(cb, nb, pb):
                def phi_g():
                    after(pe, cH_done, nb, 1)
                    after(pe, cL_done, nb, 1)
                    after(pe, V_done, nb, 0)
                    if cb is not None:
                        after(pe, out_done, cb, 0)
                    for m in range(KN):
                        last = product(CB[m // 2][:, (m % 2) * 256:(m % 2) * 256 + 256], KC,
                                       lambda a, k: ck[:, a, k, m * P:(m + 1) * P], lambda b, k: wpg[:, b, k, :])
                        if m % 2:
                            last.then_inc(pg_full[0], 1)

                def theta():
                    after(pe, xH_done, nb, 1)
                    after(pe, xL_done, nb, 1)
                    after(pe, mL_done, nb, 0)
                    if isinstance(nb, int) and nb == 0:
                        pe.wait_ge(wwT_done[0], 2)
                    product(EB[:, :], KC, lambda a, k: thw[:, a, k, :], lambda b, k: xk[:, b, k, :]
                            ).then_inc(th_full[0], 1)

                def a_transposed():
                    after(pe, xhat_done, nb, 2)
                    after(pe, max_done, nb, 0)
                    for d in range(KN):
                        for s in range(KC):
                            last = pe.transpose(DB[d // 2][:, (d % 2) * C + s * P:(d % 2) * C + (s + 1) * P],
                                                xhat[:, s, d * P:(d + 1) * P], ident[:, :])
                        if d % 2:
                            last.then_inc(aT_full[0], 1)

                def m_product():
                    after(pe, pgL_done, nb, 2)
                    after(pe, thL_done, nb, 1)
                    for m in range(KN):
                        for a in range(2):
                            last = pe.matmul(EB[:, 0:2 * P], gpv[:, m, 1, a, :],
                                             gpv[:, m, 0, :, :].rearrange("p a c -> p (a c)"),
                                             start=(m == 0 and a == 0), stop=(m == KN - 1 and a == 1))
                    last.then_inc(M_full[0], 1)

                def a_product():
                    after(pe, ML_done, nb, 1)
                    product(EB[:, 0:C], 1, lambda a, k: ms[:, a, :], lambda b, k: wwT[:, b, :]).then_inc(A_full[0], 1)

                def w_y():
                    after(pe, AL_done, nb, 1)
                    for i in range(KC):
                        product(CB[i][:, :], 1, lambda a, k: as_[:, a, i * P:(i + 1) * P],
                                lambda b, k: ths[:, b, :]).then_inc(wy_full[0], 1)

                def x1_transposed():
                    after(pe, x1_done, nb, 2)
                    for d in range(KN):
                        for s in range(KC):
                            last = pe.transpose(CB[d // 2][:, (d % 2) * C + s * P:(d % 2) * C + (s + 1) * P],
                                                x1[:, s, d * P:(d + 1) * P], ident[:, :])
                        if d % 2:
                            last.then_inc(x1T_full[0], 1)

                def k_tile(g):
                    if g == 0:
                        pe.wait_ge(w_low[0], 1) if isinstance(nb, int) and nb == 0 else None
                        after(pe, aL_done, nb, 2)
                    last = product(DB[g // 2][:, (g % 2) * C:(g % 2) * C + C], KN,
                                   lambda a, k: wk[:, a, k, g * P:(g + 1) * P], lambda b, k: aT[:, b, k, :])
                    if g % 2:
                        last.then_inc(K_full[0], 1)

                def q_tile(g):
                    if g == 0:
                        pe.wait_ge(w_low[0], 2) if isinstance(nb, int) and nb == 0 else None
                        after(pe, x1TL_done, nb, 2)
                    if g % 2 == 0:
                        after(pe, KL_done, nb, g // 2 + 1)
                    last = product(DB[g // 2][:, (g % 2) * C:(g % 2) * C + C], KN,
                                   lambda a, k: wq[:, a, k, g * P:(g + 1) * P], lambda b, k: x1T[:, b, k, :])
                    if g % 2:
                        last.then_inc(Q_full[0], 1)

                def v_tile(i):
                    if i == 0:
                        pe.wait_ge(w_low[0], 3) if isinstance(nb, int) and nb == 0 else None
                    product(CB[i][:, :], KN, lambda a, k: aT[:, a, k, i * P:(i + 1) * P],
                            lambda b, k: wv[:, b, k, :]).then_inc(V_full[0], 1)

                def scores(n):
                    if n == 0:
                        after(pe, maskrow_in, nb, 16)
                        pe.wait_ge(stack_set[0], 2) if isinstance(nb, int) and nb == 0 else None
                    if n % 8 == 0:
                        after(pe, half_in[n // 8], nb, 24 * 16)
                    if n < 2:
                        after(pe, QL_done, nb, n + 1)
                    else:
                        after(pe, max_done, nb, n - 1)
                    for t in range(2):
                        last = pe.matmul(DB[n % 2][:, t * C:(t + 1) * C], qst[0:R_MASK + 1, n, t * P:(t + 1) * P],
                                         kst[0:R_MASK + 1, n, :], start=True, stop=True)
                    last.then_inc(pre_full[0], 1)

                def scores_t(k):
                    if cb is None:
                        return
                    if k == 0:
                        after(pe, mrow_in, cb, 32)
                    after(pe, exp_done, cb, max(k - 1, 0))
                    n = STN[k]
                    for s in range(2):
                        last = pe.matmul(ST[k % 2][:, s * C:(s + 1) * C], kst[0:R_ALL, n, s * P:(s + 1) * P],
                                         qst[0:R_ALL, n, :], start=True, stop=True)
                    last.then_inc(ST_full[0], 1)

                def attend(g):
                    if cb is None:
                        return
                    if g == 0:
                        after(pe, V_done, cb, 2)
                    after(pe, exp_done, cb, 4 * g + 4)
                    after(pe, o32_done, cb, g)
                    for part in range(2):
                        for s in range(2):
                            for j in range(4):
                                h = 4 * g + j
                                left = ones[:, :] if part else vt[:, s, DH * h:DH * h + DH]
                                last = pe.matmul(PV[DH * j:DH * j + DH, part * C:(part + 1) * C], left,
                                                 pt[:, (g % 2) * 4 + j, s * C:(s + 1) * C],
                                                 start=(s == 0), stop=(s == 1))
                    last.then_inc(PV_full[0], 1)

                def o_part(n):
                    jobs = range(24 * n // H, 24 * (n + 1) // H)
                    for q in jobs:
                        i, w = divmod(q, 12)
                        if q == 0:
                            if nb is not None:
                                after(pe, V_done, nb, 2)
                            after(pe, oL_done, cb, 2)
                        last = product(CB[i][:, :], KN, lambda a, k: os_[:, a, k, i * P:(i + 1) * P],
                                       lambda b, k: wo[:, b, k, :], only=(w,))
                        if w == 11:
                            last.then_inc(O_full[0], 1)

                work = {k: [] for k in range(-1, H + 1)}
                if nb is not None:
                    work[-1] = [phi_g, theta]
                    work[0] = [a_transposed]
                    work[2] = [m_product]
                    work[4] = [a_product]
                    work[6] = [lambda: k_tile(0)]
                    work[7] = [lambda: k_tile(1), w_y]
                    work[8] = [lambda: k_tile(2)]
                    work[10] = [x1_transposed, lambda: k_tile(3)]
                    work[12] = [lambda: q_tile(0)]
                    work[14] = [lambda: q_tile(1)]
                    work[15] = [lambda: q_tile(2), lambda: q_tile(3)]
                    work[16] = [lambda: v_tile(0), lambda: v_tile(1)]
                for g in range(G):
                    work[4 * g + 5 if g < 3 else 15].append(lambda g=g: attend(g))
                for k in range(-1, H + 1):
                    if 0 <= k < H:
                        scores_t(k)
                    for job in work[k]:
                        job()
                for n in range(H):
                    if nb is not None:
                        scores(n)
                    if cb is not None:
                        o_part(n)
                if nb is not None:
                    after(pe, max_done, nb, H)
                    for t in range(2):
                        last = pe.transpose(EB[0:H, t * P:(t + 1) * P], mx[:, t, :], ident[:, :])
                    last.then_inc(mT_full[0], 1)

            turn(None, 0, 1)
            pe.wait_ge(w_low[0], 4)
            turn(0, 1, 2)
            with pe.Fori(1, B - 2) as i:
                turn(i, i + 1, i + 2)
            turn(B - 2, B - 1, None)
            turn(B - 1, None, None)


def kernel(**inputs):
    import numpy as np
    import concourse.bacc as bacc
    from concourse.bass_utils import run_bass_kernel_spmd

    a = {k: np.asarray(v) for k, v in inputs.items()}

    def by_partition(name):
        return a[name].reshape(-1, 128).T

    cols = np.concatenate([by_partition(n) for n in (
        "L0_xattn_theta_b", "L0_xattn_bn_gamma", "L0_xattn_bn_beta", "L0_xattn_bn_mean", "L0_xattn_bn_var",
        "L0_xattn_w_b", "L1_xattn_ln_gamma", "L1_xattn_ln_beta")]
        + [np.broadcast_to(a["L1_xattn_gate"].reshape(1, 1), (128, 1))], axis=1)
    arrays = {
        "x": a["x"],
        "ctx2": a["ctx_2048"],
        "mask": a["mask_BxS2_bf1"].view(np.uint8),
        "wpgT": np.concatenate([a["L0_xattn_phi_w"].T, a["L0_xattn_g_w"].T], axis=1),
        "thT": a["L0_xattn_theta_w"].T,
        "ww": a["L0_xattn_w_w"],
        "cols": cols,
        "pgb": np.broadcast_to(np.concatenate([a["L0_xattn_phi_b"], a["L0_xattn_g_b"]])[None, :], (128, 256)),
        "wkT": a["L1_xattn_Wk"].T,
        "wqT": a["L1_xattn_Wq"].T,
        "wvT": a["L1_xattn_Wv"].T,
        "woT": a["L1_xattn_Wo"].T,
    }
    arrays = {k: np.ascontiguousarray(v) for k, v in arrays.items()}
    nc = bacc.Bacc("TRN2", target_bir_lowering=False, num_devices=1)
    args = [nc.dram_tensor(k, v.shape, mybir.dt.from_np(v.dtype), kind="ExternalInput").ap()
            for k, v in arrays.items()]
    B, C, N = a["x"].shape
    args.append(nc.dram_tensor("mask_bias", (B, C), F32, kind="Internal").ap())
    args.append(nc.dram_tensor("out", (B, C, N), F32, kind="ExternalOutput").ap())
    two_layer_cross_attention(nc, *args)
    r = run_bass_kernel_spmd(nc, [arrays], core_ids=[0])
    return r.results[0]["out"]
```

```python
from contextlib import ExitStack

import concourse.bass as bass
from concourse import mybir

F32 = mybir.dt.float32
F32R = mybir.dt.float32r
U8 = mybir.dt.uint8
ALU = mybir.AluOpType
ACT = mybir.ActivationFunctionType
AX = mybir.AxisListType

P = 128
LN_EPS = 1e-5
BN_EPS = 1e-5


def two_layer_cross_attention(
    nc, x, ctx2, mask, wpgT, thT, ww, cols, pgb, wkT, wqT, wvT, woT, mask_bias, out,
):
    B, C, N = x.shape
    CI = thT.shape[1]
    H = 16
    DH = N // H
    KC = C // P
    KN = N // P
    G = H // 4
    RQ = 3 * DH
    R_MASK, R_M = RQ, RQ + 1
    R_ALL = RQ + 3
    SCALE = float(DH) ** -0.5
    assert C == 256 and N == 512 and CI == P and DH == 32

    V_THB, V_GAM, V_BET, V_MEAN, V_VAR, V_WB, V_LG, V_LB, V_GATE = 0, 1, 3, 5, 7, 9, 11, 15, 19
    NV = 20

    with ExitStack() as ctx:
        def sb(name, shape, dt=F32):
            return ctx.enter_context(nc.sbuf_tensor(name, shape, dt))

        def bank(name):
            return ctx.enter_context(nc.psum_tensor(name, [P, 512], F32))

        per = {}

        def sem(name, each_sample):
            s = ctx.enter_context(nc.semaphore(name))
            per[name] = each_sample
            return (s, name)

        def after(eng, s, sample, k):
            value = per[s[1]] * sample + k
            if isinstance(value, int) and value <= 0:
                return
            eng.wait_ge(s[0], value)

        def after_plain(eng, s, sample, k):
            if not isinstance(sample, int):
                eng.wait_ge(vec_in[0], 48)
            after(eng, s, sample, k)

        wpg = sb("wpg", [P, 2, KC, 2 * CI], F32R)
        thw = sb("thw", [P, 2, KC, CI], F32R)
        wwT = sb("wwT", [P, 2, C], F32R)
        wk = sb("wk", [P, 2, KN, N], F32R)
        wq = sb("wq", [P, 2, KN, N], F32R)
        wv = sb("wv", [P, 2, KN, N], F32R)
        wo = sb("wo", [P, 2, KN, N], F32R)
        vec = sb("vec", [P, NV])
        bias_pg = sb("bias_pg", [P, 2 * CI])
        ident = sb("ident", [P, P])
        ones = sb("ones", [P, DH])
        neg_half = sb("neg_half", [P, 2])
        bn_scale = sb("bn_scale", [P, KC])
        bn_shift = sb("bn_shift", [P, KC])
        bn_tmp = sb("bn_tmp", [P, KC])
        gate_t = sb("gate_t", [P, 1])
        mask8 = sb("mask8", [B, C], U8)
        mask_row = sb("mask_row", [B, C], F32R)

        xin = sb("xin", [P, KC, N])
        cin = sb("cin", [P, KC, N])
        xs = sb("xs", [P, 2, KC * N], F32R)
        cs = sb("cs", [P, 2, KC * N], F32R)
        pg32 = sb("pg32", [P, KN, 2 * CI])
        gp = sb("gp", [P, 2 * KC * N], F32R)
        ks = sb("ks", [P, 2, G, C], F32R)
        m32 = sb("m32", [P, 2, P])
        ms = sb("ms", [P, 2, P], F32R)
        as_ = sb("as_", [P, 2, C], F32R)
        ths = sb("ths", [P, 2, N], F32R)
        x1 = sb("x1", [P, KC, N])
        res = sb("res", [P, KC, N])
        a32 = sb("a32", [P, KN, C])
        kst = sb("kst", [P, H, C], F32R)
        qst = sb("qst", [P, H, C], F32R)
        vt = sb("vt", [P, KC, N])
        pt = sb("pt", [P, 8, 2 * C])
        rec = sb("rec", [P, C])
        pts = sb("pts", [P, 4, C])
        os_ = sb("os_", [P, 2, G, C], F32R)
        mx = sb("mx", [P, 2, H])
        mrow = sb("mrow", [H, 2, C], F32R)
        st6 = sb("st6", [P, KC, 6])
        mv = sb("mv", [P, KC, 2])
        ve, ve2, dsq, mean = (sb(n, [P, KC]) for n in ("ve", "ve2", "dsq", "mean"))
        var_eps = sb("var_eps", [P, KC])
        rstd = sb("rstd", [P, KC])

        o32 = a32
        x1T = xs[:, :, :].rearrange("p a (k t) -> p a k t", k=KN)
        aT = cs[:, :, :].rearrange("p a (k t) -> p a k t", k=KN)
        xk = xs[:, :, :].rearrange("p a (k n) -> p a k n", k=KC)
        ck = cs[:, :, :].rearrange("p a (k n) -> p a k n", k=KC)
        gpv = gp[:, :].rearrange("p (m w a c) -> p m w a c", m=KN, w=2, a=2)
        qs = gp[:, :].rearrange("p (a g t) -> p a g t", a=2, g=G)
        m_bank_t = lambda b_: b_[:, :].rearrange("p (a c) -> p a c", a=2)

        ST = [bank("ST0"), bank("ST1")]
        PV = bank("PV")
        CB = [bank("C0"), bank("C1")]
        DB = [bank("D0"), bank("D1")]
        EB = bank("E")

        vec_in = sem("vec_in", 0)
        stage_in = [sem(f"stage_in{i}", 0) for i in range(6)]
        const_done = sem("const_done", 0)
        stack_set = sem("stack_set", 0)
        ident_set = sem("ident_set", 0)
        setup_v = sem("setup_v", 0)
        setup_bn = sem("setup_bn", 0)
        setup_g = sem("setup_g", 0)
        gate_done = sem("gate_done", 0)
        w_high = sem("w_high", 0)
        w_low = sem("w_low", 0)
        wk_low = sem("wk_low", 0)
        small_high = sem("small_high", 0)
        small_low = sem("small_low", 0)
        ww_scaled = sem("ww_scaled", 0)
        wwT_full = sem("wwT_full", 0)
        wwT_done = sem("wwT_done", 0)
        bias_stored = sem("bias_stored", 0)

        x_in, c_in = sem("x_in", 16), sem("c_in", 16)
        half_in = [sem(f"half{i}_in", 2 * 5 * 16) for i in range(2)]
        k_moved = [sem(f"k_moved{i}", 4) for i in range(2)]
        q_moved = [sem(f"q_moved{i}", 4) for i in range(2)]
        maskrow_in, mrow_in, stored = sem("maskrow_in", 16), sem("mrow_in", 32), sem("stored", 16)

        pg_full, th_full, aT_full = sem("pg_full", 2), sem("th_full", 1), sem("aT_full", 2)
        M_full, A_full, wy_full, x1T_full = sem("M_full", 1), sem("A_full", 1), sem("wy_full", 2), sem("x1T_full", 2)
        K_full, Q_full, V_full = sem("K_full", 2), sem("Q_full", 2), sem("V_full", 2)
        pre_full, mT_full = sem("pre_full", H), sem("mT_full", 1)
        ST_full, PV_full, O_full = sem("ST_full", H), sem("PV_full", G), sem("O_full", 2)

        pg32_done, pgH_done, pgL_done = sem("pg32_done", 2), sem("pgH_done", 2), sem("pgL_done", 2)
        thH_done, thL_done = sem("thH_done", 1), sem("thL_done", 1)
        a32_done, aH_done, aL_done = sem("a32_done", 4), sem("aH_done", 2), sem("aL_done", 2)
        m32_done, MH_done, ML_done = sem("m32_done", 2), sem("MH_done", 1), sem("ML_done", 1)
        AH_done, AL_done = sem("AH_done", 1), sem("AL_done", 1)
        x1_done, x1TH_done, x1TL_done = sem("x1_done", 2), sem("x1TH_done", 2), sem("x1TL_done", 2)
        KH_done, KL_done = sem("KH_done", 2), sem("KL_done", 2)
        QH_done, QL_done = sem("QH_done", 2), sem("QL_done", 2)
        V_done = sem("V_done", 2)
        max_done, mH_done, mL_done = sem("max_done", H), sem("mH_done", 1), sem("mL_done", 1)
        pts_done = sem("pts_done", H)
        exp_done, rec_done, o32_done = sem("exp_done", H), sem("rec_done", G), sem("o32_done", G)
        oH_done, oL_done, out_done = sem("oH_done", 2), sem("oL_done", 2), sem("out_done", 2)
        res_done = sem("res_done", 1)
        st6_done, mv_done, ve_done, rstd_done, xhat_done = (
            sem("st6_done", 2), sem("mv_done", 5), sem("ve_done", 1), sem("rstd_done", 1), sem("xhat_done", 2))
        mean_done = sem("mean_done", 1)
        xH_done, xL_done = sem("xH_done", 1), sem("xL_done", 1)
        cH_done, cL_done = sem("cH_done", 1), sem("cL_done", 1)

        small = pg32[:, :, :].rearrange("p a b -> p (a b)")
        s_wpg = small[:, 0:512].rearrange("p (k n) -> p k n", k=KC)
        s_th = small[:, 512:768].rearrange("p (k n) -> p k n", k=KC)
        s_ww = small[:, 768:1024].rearrange("p (k n) -> p k n", k=KC)
        stage = [pt[:, 4 * i:4 * i + 4, :] for i in range(2)]
        big = [(wk, wkT), (wq, wqT), (wv, wvT), (wo, woT)]

        STN = [8 * (k // 8) + 2 * (k % 4) + (k % 8) // 4 for k in range(H)]

        block = ctx.enter_context(nc.Block())

        @block.sync
        def _(sp):
            def load_c(s):
                after_plain(sp, aT_full, s, 0)
                sp.dma_start(cin[:, :, :], ctx2[s].rearrange("(k p) n -> p k n", p=P)).then_inc(c_in[0], 16)

            def load_x(s):
                after_plain(sp, x1_done, s, 0)
                after_plain(sp, xL_done, s, 0)
                sp.dma_start(xin[:, :, :], x[s].rearrange("(k p) n -> p k n", p=P)).then_inc(x_in[0], 16)

            def low_rows(s, half, dst, low, row, done):
                after_plain(sp, done, s, half + 1)
                d = dst[:, :, :].rearrange("p (f j g) t -> p f j g t", f=2, j=4)
                for j in range(4):
                    sp.dma_start(d[row:row + DH, half, j, :, :].bitcast(F32),
                                 low[DH * j:DH * j + DH, 2 * half:2 * half + 2, :].bitcast(F32)
                                 ).then_inc(half_in[half][0], 16)

            def high_again(s, half, dst, row, moved):
                after_plain(sp, moved[half], s, 4)
                sp.dma_start(dst[row:row + DH, 8 * half:8 * half + 8, :].bitcast(F32),
                             dst[0:DH, 8 * half:8 * half + 8, :].bitcast(F32)).then_inc(half_in[half][0], 16)

            def stack_k(s, half):
                after_plain(sp, ST_full, s, 8 * half - 8)
                low_rows(s, half, kst, ks[:, 1, :, :], 2 * DH, KL_done)
                high_again(s, half, kst, DH, k_moved)

            def stack_q(s, half):
                low_rows(s, half, qst, qs[:, 1, :, :], DH, QL_done)
                high_again(s, half, qst, 2 * DH, q_moved)

            def load_weight(n):
                if n >= 2:
                    sp.wait_ge(w_high[0], n - 1)
                    sp.wait_ge((wk_low if n == 2 else w_low)[0], 1)
                sp.dma_start(stage[n % 2], big[n][1].rearrange("(k p) n -> p k n", p=P)).then_inc(stage_in[n][0], 16)

            load_c(0)
            sp.dma_start(small[:, 0:512], wpgT.rearrange("(k p) n -> p k n", p=P)).then_inc(stage_in[4][0], 16)
            load_x(0)
            sp.dma_start(vec[:, :], cols).then_inc(vec_in[0], 16)
            sp.dma_start(s_th, thT.rearrange("(k p) n -> p k n", p=P)).then_inc(stage_in[5][0], 16)
            sp.dma_start(s_ww, ww.rearrange("(k p) n -> p k n", p=P)).then_inc(stage_in[5][0], 16)
            sp.dma_start(bias_pg[:, :], pgb).then_inc(vec_in[0], 16)
            load_weight(0)
            load_weight(1)
            sp.dma_start(mask8[:, :], mask).then_inc(vec_in[0], 16)
            sp.wait_ge(setup_v[0], 1)
            sp.dma_start(mask_bias, mask_row[:, :].bitcast(F32)).then_inc(bias_stored[0], 16)
            load_weight(2)
            load_c(1)
            sp.wait_ge(bias_stored[0], 16)

            def turn(cb, nb, pb):
                if pb is not None and cb is not None:
                    load_c(pb)
                if nb is not None:
                    stack_k(nb, 0)
                    if cb is None:
                        load_weight(3)
                    if pb is not None:
                        load_x(pb)
                    stack_q(nb, 0)
                    stack_k(nb, 1)
                    if isinstance(nb, int) and nb == 0:
                        sp.wait_ge(stack_set[0], 2)
                    sp.dma_start(kst[R_MASK:R_MASK + 1, :, :].bitcast(F32),
                                 mask_bias[nb].rearrange("(o n) -> o n", o=1).unsqueeze(1).to_broadcast([1, H, C])
                                 ).then_inc(maskrow_in[0], 16)
                    stack_q(nb, 1)
                    for a, s in enumerate((mH_done, mL_done)):
                        after_plain(sp, s, nb, 1)
                        sp.dma_start(qst[R_M + a:R_M + a + 1, :, :].bitcast(F32), mrow[:, a, :].bitcast(F32)).then_inc(mrow_in[0], 16)
                if cb is not None:
                    after_plain(sp, out_done, cb, 2)
                    sp.dma_start(out[cb].rearrange("(k p) n -> p k n", p=P), res[:, :, :]).then_inc(stored[0], 16)

            turn(None, 0, 1)
            turn(0, 1, 2)
            with sp.Fori(1, B - 2) as i:
                turn(i, i + 1, i + 2)
            turn(B - 2, B - 1, None)
            turn(B - 1, None, None)
            after_plain(sp, stored, B, 0)

        @block.gpsimd
        def _(pool):
            pool.memset(ident[:, :], 0.0).then_inc(ident_set[0], 1)
            pool.memset(ones[:, :], 1.0).then_inc(const_done[0], 1)
            pool.memset(neg_half[:, :], -0.5).then_inc(const_done[0], 1)
            pool.wait_ge(ident_set[0], 1)
            pool.affine_select(out=ident[:, :], in_=ident[:, :], compare_op=ALU.not_equal, fill=1.0,
                               base=0, pattern=[[-1, P]], channel_multiplier=1).then_inc(const_done[0], 1)

            def make_rstd(s):
                after(pool, ve_done, s, 1)
                pool.tensor_tensor(rstd[:, :], var_eps[:, :], neg_half[:, :], ALU.pow).then_inc(rstd_done[0], 1)

            def x_low(s):
                after(pool, xH_done, s, 1)
                pool.tensor_tensor(xs[:, 1, :], xin[:, :, :].rearrange("p k n -> p (k n)"),
                                   xs[:, 0, :].bitcast(F32), ALU.subtract).then_inc(xL_done[0], 1)

            def c_low(s):
                after(pool, cH_done, s, 1)
                pool.tensor_tensor(cs[:, 1, :], cin[:, :, :].rearrange("p k n -> p (k n)"),
                                   cs[:, 0, :].bitcast(F32), ALU.subtract).then_inc(cL_done[0], 1)

            pool.wait_ge(const_done[0], 3)
            make_rstd(0)
            pool.wait_ge(setup_bn[0], 1)
            pool.tensor_tensor(bn_tmp[:, :], bn_scale[:, :], neg_half[:, :], ALU.pow).then_inc(setup_g[0], 1)
            x_low(0)

            def set_rows(stack, value):
                pool.memset(stack[RQ:P, :, :].bitcast(F32), value).then_inc(stack_set[0], 1)
                pool.wait_ge(stack_set[0], 1 if stack is kst else 2)

            def cut_low(n):
                pool.wait_ge(w_high[0], n + 1)
                w = big[n][0]
                pool.tensor_tensor(w[:, 1, :, :], stage[n % 2], w[:, 0, :, :].bitcast(F32),
                                   ALU.subtract).then_inc(w_low[0], 1)

            pool.wait_ge(xL_done[0], 1)
            set_rows(kst, -1.0)

            def turn(cb, nb, pb):
                def out_low(i):
                    after(pool, oH_done, cb, i + 1)
                    pool.tensor_tensor(os_[:, 1, 2 * i:2 * i + 2, :], o32[:, 2 * i:2 * i + 2, :],
                                       os_[:, 0, 2 * i:2 * i + 2, :].bitcast(F32),
                                       ALU.subtract).then_inc(oL_done[0], 1)

                if nb is not None:
                    for i in range(2):
                        after(pool, pgH_done, nb, i + 1)
                        src = pg32[:, 2 * i:2 * i + 2, :].rearrange("p m (w c) -> p m w c", w=2)
                        pool.tensor_tensor(gpv[:, 2 * i:2 * i + 2, :, 1, :], src,
                                           gpv[:, 2 * i:2 * i + 2, :, 0, :].bitcast(F32),
                                           ALU.subtract).then_inc(pgL_done[0], 1)
                if cb is None:
                    for n in range(1, 3):
                        cut_low(n)
                    pool.wait_ge(w_low[0], 2)
                    set_rows(qst, 1.0)
                    cut_low(3)
                else:
                    for k in range(H):
                        after(pool, exp_done, cb, k + 1)
                        if k % 4 == 0:
                            after(pool, PV_full, cb, k // 4)
                        pool.tensor_tensor(pts[:, k % 4, :], pt[:, k % 8, 0:C], pt[:, k % 8, C:2 * C],
                                           ALU.add).then_inc(pts_done[0], 1)
                        if k == 11:
                            out_low(0)
                    out_low(1)
                if pb is not None:
                    make_rstd(pb)
                    c_low(pb)
                    x_low(pb)

            turn(None, 0, 1)
            turn(0, 1, 2)
            with pool.Fori(1, B - 2) as i:
                turn(i, i + 1, i + 2)
            turn(B - 2, B - 1, None)
            turn(B - 1, None, None)

        @block.scalar
        def _(act):
            def x_high(s):
                after(act, x_in, s, 16)
                after(act, Q_full, s, 0)
                act.activation(xs[:, 0, :], xin[:, :, :].rearrange("p k n -> p (k n)"), ACT.Copy).then_inc(xH_done[0], 1)

            def c_high(s):
                after(act, c_in, s, 16)
                after(act, V_full, s, 0)
                act.activation(cs[:, 0, :], cin[:, :, :].rearrange("p k n -> p (k n)"), ACT.Copy).then_inc(cH_done[0], 1)

            def a_transposed_out(s, cb):
                after(act, aL_done, s, 0)
                if cb is not None:
                    after(act, oL_done, cb, 2)
                for d in range(KN):
                    after(act, aT_full, s, d // 2 + 1)
                    act.activation(a32[:, d, :], DB[d // 2][:, (d % 2) * C:(d % 2) * C + C], ACT.Identity,
                                   bias=vec[:, V_LB + d:V_LB + d + 1],
                                   scale=vec[:, V_LG + d:V_LG + d + 1]).then_inc(a32_done[0], 1)

            def cut_high(n):
                act.wait_ge(stage_in[n][0], 16)
                act.activation(big[n][0][:, 0, :, :], stage[n % 2], ACT.Copy).then_inc(w_high[0], 1)

            c_high(0)
            x_high(0)
            act.wait_ge(vec_in[0], 48)
            cut_high(0)
            a_transposed_out(0, None)
            act.activation(gate_t[:, :], vec[:, V_GATE:V_GATE + 1], ACT.Tanh).then_inc(gate_done[0], 1)

            def turn(cb, nb, pb):
                def exp(k):
                    if cb is None:
                        return
                    if k % 4 == 0:
                        after(act, PV_full, cb, max(k // 4 - 1, 0))
                    if k == 0 and isinstance(cb, int) and cb == 0:
                        act.wait_ge(w_low[0], 3)
                    after(act, ST_full, cb, k + 1)
                    act.activation(pt[:, k % 8, :], ST[k % 2][:, :], ACT.Exp, scale=SCALE).then_inc(exp_done[0], 1)

                def keep_x1():
                    after(act, stored, cb, 0)
                    after(act, x1_done, cb, 2)
                    act.activation(res[:, :, :], x1[:, :, :], ACT.Copy).then_inc(res_done[0], 1)

                def a_high(i):
                    after(act, a32_done, nb, 2 * i + 2)
                    after(act, pg_full, nb, 2)
                    act.activation(aT[:, 0, 2 * i:2 * i + 2, :], a32[:, 2 * i:2 * i + 2, :], ACT.Copy
                                   ).then_inc(aH_done[0], 1)

                def theta_high():
                    after(act, th_full, nb, 1)
                    act.activation(ths[:, 0, :], EB[:, :], ACT.Identity,
                                   bias=vec[:, V_THB:V_THB + 1]).then_inc(thH_done[0], 1)

                def high(full, bank_, dst, i, done, free, free_k):
                    after(act, free, nb, free_k)
                    after(act, full, nb, i + 1)
                    act.activation(dst[:, 0, 2 * i:2 * i + 2, :], bank_[:, :].rearrange("p (a t) -> p a t", a=2),
                                   ACT.Copy).then_inc(done[0], 1)

                k_high = lambda i: high(K_full, DB[i], ks, i, KH_done, pre_full, 0)
                q_high = lambda i: high(Q_full, DB[i], qs, i, QH_done, M_full, 1)
                x1T_high = lambda i: high(x1T_full, CB[i], x1T, i, x1TH_done, th_full, 1)

                def move(dst, src, half, j, done, moved):
                    after(act, ST_full, nb, 8 * half - 8)
                    after(act, done, nb, half + 1)
                    n = 8 * half + 2 * j
                    act.activation(dst[0:DH, n:n + 2, :], src[DH * j:DH * j + DH, 0, 2 * half:2 * half + 2, :].bitcast(F32),
                                   ACT.Copy).then_inc(moved[half][0], 1)

                k_move = lambda half, j: move(kst, ks, half, j, KH_done, k_moved)
                q_move = lambda half, j: move(qst, qs, half, j, QH_done, q_moved)

                def values(i):
                    if cb is not None:
                        after(act, PV_full, cb, 4)
                    after(act, V_full, nb, i + 1)
                    act.activation(vt[:, i, :], CB[i][:, :], ACT.Copy).then_inc(V_done[0], 1)

                S1, S2 = nb is not None, cb is not None
                if S1:
                    a_high(0)
                    a_high(1)
                    theta_high()
                    if cb is None:
                        cut_high(1)
                for k in range(4):
                    exp(k)
                if S1:
                    k_high(0)
                if S2:
                    keep_x1()
                for k in range(4, 8):
                    exp(k)
                if S1:
                    k_high(1)
                    x1T_high(0)
                    x1T_high(1)
                    if cb is None:
                        cut_high(2)
                for k in range(8, 12):
                    exp(k)
                    if S1:
                        k_move(0, k - 8)
                if S1:
                    q_high(0)
                    q_move(0, 0)
                    q_move(0, 1)
                exp(12)
                if S1:
                    q_move(0, 2)
                    q_move(0, 3)
                exp(13)
                exp(14)
                exp(15)
                if S1:
                    q_high(1)
                    for j in range(4):
                        k_move(1, j)
                    for j in range(4):
                        q_move(1, j)
                    values(0)
                    values(1)
                if pb is not None:
                    if cb is None:
                        cut_high(3)
                    c_high(pb)
                    x_high(pb)
                    a_transposed_out(pb, cb)

            turn(None, 0, 1)
            turn(0, 1, 2)
            with act.Fori(1, B - 2) as i:
                turn(i, i + 1, i + 2)
            turn(B - 2, B - 1, None)
            turn(B - 1, None, None)

        @block.vector
        def _(dve):
            def stats(s):
                after(dve, c_in, s, 16)
                for k in range(KC):
                    dve.bn_stats(st6[:, k, :], cin[:, k, :]).then_inc(st6_done[0], 1)
                after(dve, st6_done, s, KC)
                dve.tensor_tensor(mv[:, :, 0], st6[:, :, 1], st6[:, :, 4], ALU.add).then_inc(mv_done[0], 1)
                dve.tensor_tensor(mv[:, :, 1], st6[:, :, 1], st6[:, :, 4], ALU.subtract).then_inc(mv_done[0], 1)
                dve.tensor_tensor(ve[:, :], st6[:, :, 2], st6[:, :, 5], ALU.add).then_inc(mv_done[0], 1)
                after(dve, mv_done, s, 3)
                dve.tensor_scalar(mean[:, :], mv[:, :, 0], 0.5, None, ALU.mult).then_inc(mean_done[0], 1)
                dve.tensor_scalar(ve2[:, :], ve[:, :], 1.0 / N, LN_EPS, ALU.mult, ALU.add).then_inc(mv_done[0], 1)
                dve.scalar_tensor_tensor(out=dsq[:, :], in0=mv[:, :, 1], scalar=0.25, in1=mv[:, :, 1],
                                         op0=ALU.mult, op1=ALU.mult).then_inc(mv_done[0], 1)
                after(dve, mv_done, s, 5)
                dve.tensor_tensor(var_eps[:, :], ve2[:, :], dsq[:, :], ALU.add).then_inc(ve_done[0], 1)

            def normalise(s):
                after(dve, cH_done, s, 1)
                after(dve, cL_done, s, 1)
                after(dve, rstd_done, s, 1)
                after(dve, mean_done, s, 1)
                for k in range(KC):
                    dve.tensor_scalar(cin[:, k, :], cin[:, k, :], mean[:, k:k + 1], rstd[:, k:k + 1],
                                      ALU.subtract, ALU.mult).then_inc(xhat_done[0], 1)

            stats(0)
            dve.wait_ge(stage_in[4][0], 16)
            dve.tensor_copy(wpg[:, 0, :, :], s_wpg).then_inc(small_high[0], 1)
            dve.wait_ge(small_high[0], 1)
            dve.tensor_tensor(wpg[:, 1, :, :], s_wpg, wpg[:, 0, :, :].bitcast(F32), ALU.subtract).then_inc(small_low[0], 1)
            after(dve, cH_done, 0, 1)
            dve.tensor_tensor(cs[:, 1, :], cin[:, :, :].rearrange("p k n -> p (k n)"),
                              cs[:, 0, :].bitcast(F32), ALU.subtract).then_inc(cL_done[0], 1)
            dve.wait_ge(vec_in[0], 48)
            dve.tensor_scalar(bn_scale[:, :], vec[:, V_VAR:V_VAR + KC], BN_EPS, None, ALU.add).then_inc(setup_bn[0], 1)
            dve.wait_ge(stage_in[5][0], 32)
            dve.tensor_copy(thw[:, 0, :, :], s_th).then_inc(small_high[0], 1)
            dve.wait_ge(small_high[0], 2)
            dve.tensor_tensor(thw[:, 1, :, :], s_th, thw[:, 0, :, :].bitcast(F32), ALU.subtract).then_inc(small_low[0], 1)
            normalise(0)
            dve.wait_ge(setup_g[0], 1)
            dve.tensor_tensor(bn_scale[:, :], bn_tmp[:, :], vec[:, V_GAM:V_GAM + KC], ALU.mult).then_inc(setup_bn[0], 1)
            dve.tensor_tensor(bn_shift[:, :], vec[:, V_WB:V_WB + KC], vec[:, V_MEAN:V_MEAN + KC],
                              ALU.subtract).then_inc(setup_bn[0], 1)
            dve.wait_ge(setup_bn[0], 3)
            dve.tensor_tensor(bn_tmp[:, :], bn_shift[:, :], bn_scale[:, :], ALU.mult).then_inc(setup_bn[0], 1)
            for k in range(KC):
                dve.tensor_scalar(s_ww[:, k, :], s_ww[:, k, :], bn_scale[:, k:k + 1], None,
                                  ALU.mult).then_inc(ww_scaled[0], 1)
            dve.wait_ge(setup_bn[0], 4)
            dve.tensor_tensor(bn_shift[:, :], bn_tmp[:, :], vec[:, V_BET:V_BET + KC], ALU.add).then_inc(setup_bn[0], 1)
            dve.tensor_scalar(rec[0:B, :], mask8[:, :], 1.0, 3e38, ALU.subtract, ALU.mult).then_inc(setup_bn[0], 1)
            dve.wait_ge(setup_bn[0], 6)
            dve.tensor_scalar(mask_row[:, :], rec[0:B, :], 1e3, None, ALU.mult).then_inc(setup_v[0], 1)
            dve.wait_ge(w_high[0], 1)
            dve.tensor_tensor(wk[:, 1, :, :], stage[0], wk[:, 0, :, :].bitcast(F32), ALU.subtract).then_inc(wk_low[0], 1)
            dve.wait_ge(wwT_full[0], 1)
            dve.tensor_copy(wwT[:, 0, :], EB[:, 0:C]).then_inc(wwT_done[0], 1)
            dve.wait_ge(wwT_done[0], 1)
            dve.tensor_tensor(wwT[:, 1, :], EB[:, 0:C], wwT[:, 0, :].bitcast(F32), ALU.subtract).then_inc(wwT_done[0], 1)
            dve.wait_ge(gate_done[0], 1)

            def turn(cb, nb, pb):
                def low(done_h, bank_, dst, hi, i, s, done):
                    after(dve, done_h, s, i + 1)
                    dve.tensor_tensor(dst, bank_[:, :].rearrange("p (a t) -> p a t", a=2), hi.bitcast(F32),
                                      ALU.subtract).then_inc(done[0], 1)

                def attended(g):
                    if cb is None:
                        return
                    if g == 0:
                        if nb is not None:
                            after(dve, aL_done, nb, 2)
                        after(dve, oL_done, cb, 0)
                    after(dve, PV_full, cb, g + 1)
                    dve.reciprocal(rec[:, :], PV[:, C:2 * C]).then_inc(rec_done[0], 1)
                    after(dve, rec_done, cb, g + 1)
                    dve.tensor_tensor(o32[:, g, :], PV[:, 0:C], rec[:, :], ALU.mult).then_inc(o32_done[0], 1)
                    if g % 2:
                        i = g // 2
                        after(dve, O_full, cb, 0)
                        after(dve, o32_done, cb, g + 1)
                        dve.tensor_copy(os_[:, 0, g - 1:g + 1, :], o32[:, g - 1:g + 1, :]).then_inc(oH_done[0], 1)

                if nb is not None:
                    after(dve, pgL_done, nb, 0)
                    for i in range(2):
                        after(dve, pg_full, nb, i + 1)
                        dve.tensor_tensor(pg32[:, 2 * i:2 * i + 2, :], CB[i][:, :].rearrange("p (m n) -> p m n", m=2),
                                          bias_pg[:, :].unsqueeze(1).to_broadcast([P, 2, 2 * CI]), ALU.add
                                          ).then_inc(pg32_done[0], 1)
                        after(dve, pg32_done, nb, i + 1)
                        dve.tensor_copy(gpv[:, 2 * i:2 * i + 2, :, 0, :],
                                        pg32[:, 2 * i:2 * i + 2, :].rearrange("p m (w c) -> p m w c", w=2)
                                        ).then_inc(pgH_done[0], 1)
                    for i in range(2):
                        after(dve, aH_done, nb, i + 1)
                        dve.tensor_tensor(aT[:, 1, 2 * i:2 * i + 2, :], a32[:, 2 * i:2 * i + 2, :],
                                          aT[:, 0, 2 * i:2 * i + 2, :].bitcast(F32), ALU.subtract).then_inc(aL_done[0], 1)
                    after(dve, thH_done, nb, 1)
                    dve.scalar_tensor_tensor(out=ths[:, 1, :], in0=EB[:, :], scalar=vec[:, V_THB:V_THB + 1],
                                             in1=ths[:, 0, :].bitcast(F32), op0=ALU.add,
                                             op1=ALU.subtract).then_inc(thL_done[0], 1)
                    after(dve, M_full, nb, 1)
                    dve.tensor_scalar(m32[:, 0, :], EB[:, 0:P], 1.0 / N, None, ALU.mult).then_inc(m32_done[0], 1)
                    after(dve, m32_done, nb, 1)
                    dve.scalar_tensor_tensor(out=m32[:, 1, :], in0=EB[:, P:2 * P], scalar=1.0 / N, in1=m32[:, 0, :],
                                             op0=ALU.mult, op1=ALU.add).then_inc(m32_done[0], 1)
                    after(dve, m32_done, nb, 2)
                    dve.tensor_copy(ms[:, 0, :], m32[:, 1, :]).then_inc(MH_done[0], 1)
                    after(dve, MH_done, nb, 1)
                    dve.tensor_tensor(ms[:, 1, :], m32[:, 1, :], ms[:, 0, :].bitcast(F32),
                                      ALU.subtract).then_inc(ML_done[0], 1)
                    after(dve, A_full, nb, 1)
                    dve.tensor_copy(as_[:, 0, :], EB[:, 0:C]).then_inc(AH_done[0], 1)
                    after(dve, AH_done, nb, 1)
                    dve.tensor_tensor(as_[:, 1, :], EB[:, 0:C], as_[:, 0, :].bitcast(F32),
                                      ALU.subtract).then_inc(AL_done[0], 1)
                k_low = lambda i: low(KH_done, DB[i], ks[:, 1, 2 * i:2 * i + 2, :], ks[:, 0, 2 * i:2 * i + 2, :],
                                      i, nb, KL_done)
                q_low = lambda i: low(QH_done, DB[i], qs[:, 1, 2 * i:2 * i + 2, :], qs[:, 0, 2 * i:2 * i + 2, :],
                                      i, nb, QL_done)
                x1T_low = lambda i: low(x1TH_done, CB[i], x1T[:, 1, 2 * i:2 * i + 2, :],
                                        x1T[:, 0, 2 * i:2 * i + 2, :], i, nb, x1TL_done)

                def sum_x1():
                    if cb is not None:
                        after(dve, res_done, cb, 1)
                    for i in range(KC):
                        after(dve, wy_full, nb, i + 1)
                        dve.scalar_tensor_tensor(out=x1[:, i, :], in0=CB[i][:, :], scalar=bn_shift[:, i:i + 1],
                                                 in1=xin[:, i, :], op0=ALU.add, op1=ALU.add).then_inc(x1_done[0], 1)

                def maximum(n):
                    after(dve, pre_full, nb, n + 1)
                    dve.tensor_reduce(mx[:, :, n], DB[n % 2][:, :].rearrange("p (a s) -> p a s", a=2),
                                      AX.X, ALU.max).then_inc(max_done[0], 1)

                def final(i):
                    after(dve, O_full, cb, i + 1)
                    after(dve, res_done, cb, 1)
                    dve.scalar_tensor_tensor(out=res[:, i, :], in0=CB[i][:, :], scalar=gate_t[:, 0:1],
                                             in1=res[:, i, :], op0=ALU.mult, op1=ALU.add).then_inc(out_done[0], 1)

                S1, S2 = nb is not None, cb is not None
                if S1:
                    k_low(0)
                if S2:
                    attended(0)
                if S1:
                    sum_x1()
                    k_low(1)
                    x1T_low(0)
                    x1T_low(1)
                if S2:
                    attended(1)
                if S1:
                    q_low(0)
                if S2:
                    attended(2)
                if S1:
                    q_low(1)
                if S2:
                    attended(3)
                if pb is not None:
                    stats(pb)
                if S1:
                    for n in range(8):
                        maximum(n)
                if S1:
                    for n in range(8, 12):
                        maximum(n)
                if S2:
                    final(0)
                if S1:
                    maximum(12)
                    maximum(13)
                if pb is not None:
                    normalise(pb)
                if S1:
                    maximum(14)
                if S2:
                    final(1)
                if S1:
                    maximum(15)
                    after(dve, mT_full, nb, 1)
                    dve.tensor_copy(mrow[:, 0, :], EB[0:H, 0:C]).then_inc(mH_done[0], 1)
                    after(dve, mH_done, nb, 1)
                    dve.tensor_tensor(mrow[:, 1, :], EB[0:H, 0:C], mrow[:, 0, :].bitcast(F32),
                                      ALU.subtract).then_inc(mL_done[0], 1)

            turn(None, 0, 1)
            turn(0, 1, 2)
            with dve.Fori(1, B - 2) as i:
                turn(i, i + 1, i + 2)
            turn(B - 2, B - 1, None)
            turn(B - 1, None, None)

        @block.tensor
        def _(pe):
            def a_transposed(s_):
                after(pe, xhat_done, s_, 2)
                for d in range(KN):
                    if d % 2 == 0:
                        after(pe, max_done, s_, d // 2 - 1)
                    for s in range(KC):
                        last = pe.transpose(DB[d // 2][:, (d % 2) * C + s * P:(d % 2) * C + (s + 1) * P],
                                            cin[:, s, d * P:(d + 1) * P], ident[:, :])
                    if d % 2:
                        last.then_inc(aT_full[0], 1)

            pe.wait_ge(const_done[0], 3)
            a_transposed(0)
            pe.wait_ge(ww_scaled[0], 2)
            for k in range(KC):
                last = pe.transpose(EB[:, k * P:(k + 1) * P], s_ww[:, k, :], ident[:, :])
            last.then_inc(wwT_full[0], 1)
            pe.wait_ge(small_low[0], 2)

            PASSES = ((0, 0), (0, 1), (1, 0))

            def product(dst, depth, left, right, only=None):
                jobs = [(k, a, b) for k in range(depth) for a, b in PASSES]
                last = None
                for n, (k, a, b) in enumerate(jobs):
                    if only is None or n in only:
                        last = pe.matmul(dst, left(a, k), right(b, k), start=(n == 0), stop=(n == len(jobs) - 1))
                return last

            def turn(cb, nb, pb):
                def phi_g():
                    after(pe, cH_done, nb, 1)
                    after(pe, cL_done, nb, 1)
                    after(pe, V_done, nb, 0)
                    for m in range(KN):
                        if cb is not None and m % 2 == 0:
                            after(pe, out_done, cb, 0) if m else after(pe, out_done, cb, -1)
                        last = product(CB[m // 2][:, (m % 2) * 256:(m % 2) * 256 + 256], KC,
                                       lambda a, k: ck[:, a, k, m * P:(m + 1) * P], lambda b, k: wpg[:, b, k, :])
                        if m % 2:
                            last.then_inc(pg_full[0], 1)

                def theta():
                    after(pe, xH_done, nb, 1)
                    after(pe, xL_done, nb, 1)
                    after(pe, mL_done, nb, 0)
                    if isinstance(nb, int) and nb == 0:
                        pe.wait_ge(wwT_done[0], 2)
                    product(EB[:, :], KC, lambda a, k: thw[:, a, k, :], lambda b, k: xk[:, b, k, :]
                            ).then_inc(th_full[0], 1)

                def m_product():
                    after(pe, pgL_done, nb, 2)
                    after(pe, thL_done, nb, 1)
                    for m in range(KN):
                        for a in range(2):
                            last = pe.matmul(EB[:, 0:2 * P], gpv[:, m, 1, a, :],
                                             gpv[:, m, 0, :, :].rearrange("p a c -> p (a c)"),
                                             start=(m == 0 and a == 0), stop=(m == KN - 1 and a == 1))
                    last.then_inc(M_full[0], 1)

                def a_product():
                    after(pe, ML_done, nb, 1)
                    product(EB[:, 0:C], 1, lambda a, k: ms[:, a, :], lambda b, k: wwT[:, b, :]).then_inc(A_full[0], 1)

                def w_y():
                    after(pe, AL_done, nb, 1)
                    for i in range(KC):
                        product(CB[i][:, :], 1, lambda a, k: as_[:, a, i * P:(i + 1) * P],
                                lambda b, k: ths[:, b, :]).then_inc(wy_full[0], 1)

                def x1_transposed():
                    after(pe, x1_done, nb, 2)
                    for d in range(KN):
                        for s in range(KC):
                            last = pe.transpose(CB[d // 2][:, (d % 2) * C + s * P:(d % 2) * C + (s + 1) * P],
                                                x1[:, s, d * P:(d + 1) * P], ident[:, :])
                        if d % 2:
                            last.then_inc(x1T_full[0], 1)

                def k_tile(g):
                    if g == 0:
                        pe.wait_ge(wk_low[0], 1) if isinstance(nb, int) and nb == 0 else None
                        after(pe, aL_done, nb, 2)
                    last = product(DB[g // 2][:, (g % 2) * C:(g % 2) * C + C], KN,
                                   lambda a, k: wk[:, a, k, g * P:(g + 1) * P], lambda b, k: aT[:, b, k, :])
                    if g % 2:
                        last.then_inc(K_full[0], 1)

                def q_tile(g):
                    if g == 0:
                        pe.wait_ge(w_low[0], 1) if isinstance(nb, int) and nb == 0 else None
                        after(pe, x1TL_done, nb, 2)
                    if g % 2 == 0:
                        after(pe, KL_done, nb, g // 2 + 1)
                    last = product(DB[g // 2][:, (g % 2) * C:(g % 2) * C + C], KN,
                                   lambda a, k: wq[:, a, k, g * P:(g + 1) * P], lambda b, k: x1T[:, b, k, :])
                    if g % 2:
                        last.then_inc(Q_full[0], 1)

                def scores(n):
                    if n == 0:
                        after(pe, maskrow_in, nb, 16)
                        pe.wait_ge(stack_set[0], 2) if isinstance(nb, int) and nb == 0 else None
                    if n % 8 == 0:
                        after(pe, half_in[n // 8], nb, 2 * 5 * 16)
                    if n < 2:
                        after(pe, QL_done, nb, n + 1)
                    else:
                        after(pe, max_done, nb, n - 1)
                    for t in range(2):
                        last = pe.matmul(DB[n % 2][:, t * C:(t + 1) * C], qst[0:R_MASK + 1, n, t * P:(t + 1) * P],
                                         kst[0:R_MASK + 1, n, :], start=True, stop=True)
                    last.then_inc(pre_full[0], 1)

                def scores_t(k):
                    if cb is None:
                        return
                    if k == 0:
                        after(pe, mrow_in, cb, 32)
                    after(pe, exp_done, cb, max(k - 1, 0))
                    n = STN[k]
                    for s in range(2):
                        last = pe.matmul(ST[k % 2][:, s * C:(s + 1) * C], kst[0:R_ALL, n, s * P:(s + 1) * P],
                                         qst[0:R_ALL, n, :], start=True, stop=True)
                    last.then_inc(ST_full[0], 1)

                def attend(g):
                    if cb is None:
                        return
                    if g == 0:
                        after(pe, V_done, cb, 2)
                    after(pe, exp_done, cb, 4 * g + 4)
                    after(pe, o32_done, cb, g)
                    for s in range(2):
                        for j in range(4):
                            h = 4 * g + j
                            pe.matmul(PV[DH * j:DH * j + DH, 0:C], vt[:, s, DH * h:DH * h + DH],
                                      pt[:, (g % 2) * 4 + j, s * C:(s + 1) * C], start=(s == 0), stop=(s == 1))
                    after(pe, pts_done, cb, 4 * g + 4)
                    for j in range(4):
                        last = pe.matmul(PV[DH * j:DH * j + DH, C:2 * C], ones[:, :], pts[:, j, :],
                                         start=True, stop=True)
                    last.then_inc(PV_full[0], 1)

                def v_matmuls(lo, hi):
                    for q in range(lo, hi):
                        i, w = divmod(q, 12)
                        last = product(CB[i][:, :], KN, lambda a, k: aT[:, a, k, i * P:(i + 1) * P],
                                       lambda b, k: wv[:, b, k, :], only=(w,))
                        if w == 11:
                            last.then_inc(V_full[0], 1)

                def o_matmuls(lo, hi):
                    for q in range(lo, hi):
                        i, w = divmod(q, 12)
                        if w == 0:
                            if isinstance(cb, int) and cb == 0:
                                pe.wait_ge(w_low[0], 3)
                            if nb is not None:
                                after(pe, V_done, nb, i + 1)
                            after(pe, oL_done, cb, 2)
                        last = product(CB[i][:, :], KN, lambda a, k: os_[:, a, k, i * P:(i + 1) * P],
                                       lambda b, k: wo[:, b, k, :], only=(w,))
                        if w == 11:
                            last.then_inc(O_full[0], 1)

                S1, S2 = nb is not None, cb is not None
                beside = {k: [] for k in range(-1, H)}
                if S1:
                    beside[-1] = [phi_g, theta]
                    beside[1] = [m_product]
                    beside[2] = [lambda: k_tile(0)]
                    beside[3] = [a_product, lambda: k_tile(1)]
                    beside[5] = [w_y]
                    beside[6] = [lambda: k_tile(2)]
                    beside[7] = [lambda: k_tile(3)]
                    beside[8] = [x1_transposed]
                    beside[10] = [lambda: q_tile(0)]
                    beside[11] = [lambda: q_tile(1)]
                    beside[12] = [lambda: q_tile(2)]
                    beside[14] = [lambda: q_tile(3)]
                if S2:
                    for g in range(G - 1):
                        beside[4 * g + 5].insert(0, lambda g=g: attend(g))
                for k in range(-1, H):
                    if k >= 0:
                        scores_t(k)
                    for job in beside[k]:
                        job()
                if S1:
                    pe.wait_ge(w_low[0], 2) if isinstance(nb, int) and nb == 0 else None
                    v_matmuls(0, 3)
                if S2:
                    attend(G - 1)
                for n in range(H):
                    if S1:
                        if n < 8:
                            v_matmuls(3 + 21 * n // 8, 3 + 21 * (n + 1) // 8)
                        scores(n)
                    if S2 and n >= 8:
                        o_matmuls(24 * (n - 8) // 7 if n < 15 else 24, min(24, 24 * (n - 7) // 7))
                if pb is not None:
                    a_transposed(pb)
                if S1:
                    after(pe, max_done, nb, H)
                    for t in range(2):
                        last = pe.transpose(EB[0:H, t * P:(t + 1) * P], mx[:, t, :], ident[:, :])
                    last.then_inc(mT_full[0], 1)

            turn(None, 0, 1)
            turn(0, 1, 2)
            with pe.Fori(1, B - 2) as i:
                turn(i, i + 1, i + 2)
            turn(B - 2, B - 1, None)
            turn(B - 1, None, None)


def kernel(**inputs):
    import numpy as np
    import concourse.bacc as bacc
    from concourse.bass_utils import run_bass_kernel_spmd

    a = {k: np.asarray(v) for k, v in inputs.items()}

    def by_partition(name):
        return a[name].reshape(-1, 128).T

    cols = np.concatenate([by_partition(n) for n in (
        "L0_xattn_theta_b", "L0_xattn_bn_gamma", "L0_xattn_bn_beta", "L0_xattn_bn_mean", "L0_xattn_bn_var",
        "L0_xattn_w_b", "L1_xattn_ln_gamma", "L1_xattn_ln_beta")]
        + [np.broadcast_to(a["L1_xattn_gate"].reshape(1, 1), (128, 1))], axis=1)
    arrays = {
        "x": a["x"],
        "ctx2": a["ctx_2048"],
        "mask": a["mask_BxS2_bf1"].view(np.uint8),
        "wpgT": np.concatenate([a["L0_xattn_phi_w"].T, a["L0_xattn_g_w"].T], axis=1),
        "thT": a["L0_xattn_theta_w"].T,
        "ww": a["L0_xattn_w_w"],
        "cols": cols,
        "pgb": np.broadcast_to(np.concatenate([a["L0_xattn_phi_b"], a["L0_xattn_g_b"]])[None, :], (128, 256)),
        "wkT": a["L1_xattn_Wk"].T,
        "wqT": a["L1_xattn_Wq"].T,
        "wvT": a["L1_xattn_Wv"].T,
        "woT": a["L1_xattn_Wo"].T,
    }
    arrays = {k: np.ascontiguousarray(v) for k, v in arrays.items()}
    nc = bacc.Bacc("TRN2", target_bir_lowering=False, num_devices=1)
    args = [nc.dram_tensor(k, v.shape, mybir.dt.from_np(v.dtype), kind="ExternalInput").ap()
            for k, v in arrays.items()]
    B, C, N = a["x"].shape
    args.append(nc.dram_tensor("mask_bias", (B, C), F32, kind="Internal").ap())
    args.append(nc.dram_tensor("out", (B, C, N), F32, kind="ExternalOutput").ap())
    two_layer_cross_attention(nc, *args)
    r = run_bass_kernel_spmd(nc, [arrays], core_ids=[0])
    return r.results[0]["out"]
```

```python
from contextlib import ExitStack

import concourse.bass as bass
from concourse import mybir

F32 = mybir.dt.float32
F32R = mybir.dt.float32r
U8 = mybir.dt.uint8
ALU = mybir.AluOpType
ACT = mybir.ActivationFunctionType
AX = mybir.AxisListType

P = 128
LN_EPS = 1e-5
BN_EPS = 1e-5
MASKED = 1e30


def two_layer_cross_attention(
    nc, x, ctx2, mask, wpgT, thT, ww, cols, pgb, wkT, wqT, wvT, woT, mask_bias, out,
):
    B, C, N = x.shape
    CI = thT.shape[1]
    H = 16
    DH = N // H
    KC = C // P
    KN = N // P
    G = H // 4
    RQ = 3 * DH
    R_MASK, R_M = RQ, RQ + 1
    R_ALL = RQ + 3
    SCALE = float(DH) ** -0.5
    assert C == 256 and N == 512 and CI == P and DH == 32

    V_THB, V_GAM, V_BET, V_MEAN, V_VAR, V_WB, V_LG, V_LB, V_GATE = 0, 1, 3, 5, 7, 9, 11, 15, 19
    NV = 20

    with ExitStack() as ctx:
        def sb(name, shape, dt=F32):
            return ctx.enter_context(nc.sbuf_tensor(name, shape, dt))

        def bank(name):
            return ctx.enter_context(nc.psum_tensor(name, [P, 512], F32))

        per = {}

        def sem(name, each_sample):
            s = ctx.enter_context(nc.semaphore(name))
            per[name] = each_sample
            return (s, name)

        def after(eng, s, sample, k):
            value = per[s[1]] * sample + k
            if isinstance(value, int) and value <= 0:
                return
            eng.wait_ge(s[0], value)

        def after_plain(eng, s, sample, k):
            if not isinstance(sample, int):
                eng.wait_ge(vec_in[0], 48)
            after(eng, s, sample, k)

        def is_first(sample):
            return isinstance(sample, int) and sample == 0

        wpg = sb("wpg", [P, 2, KC, 2 * CI], F32R)
        thw = sb("thw", [P, 2, KC, CI], F32R)
        wwT = sb("wwT", [P, 2, C], F32R)
        wk = sb("wk", [P, 2, KN, N], F32R)
        wq = sb("wq", [P, 2, KN, N], F32R)
        wv = sb("wv", [P, 2, KN, N], F32R)
        wo = sb("wo", [P, 2, KN, N], F32R)
        vec = sb("vec", [P, NV])
        bias_pg = sb("bias_pg", [P, 2 * CI])
        ident = sb("ident", [P, P])
        ones = sb("ones", [P, DH])
        neg_half = sb("neg_half", [P, 2])
        bn_scale = sb("bn_scale", [P, KC])
        bn_shift = sb("bn_shift", [P, KC])
        bn_tmp = sb("bn_tmp", [P, KC])
        gate_t = sb("gate_t", [P, 1])
        mask8 = sb("mask8", [B, C], U8)
        mask_row = sb("mask_row", [B, C], F32R)
        no_key = sb("no_key", [B, 1])

        xin = sb("xin", [P, KC, N])
        cin = sb("cin", [P, KC, N])
        xs = sb("xs", [P, 2, KC * N], F32R)
        cs = sb("cs", [P, 2, KC * N], F32R)
        pg32 = sb("pg32", [P, KN, 2 * CI])
        gp = sb("gp", [P, 2 * KC * N], F32R)
        ks = sb("ks", [P, 2, G, C], F32R)
        m32 = sb("m32", [P, 2, P])
        ms = sb("ms", [P, 2, P], F32R)
        as_ = sb("as_", [P, 2, C], F32R)
        ths = sb("ths", [P, 2, N], F32R)
        x1 = sb("x1", [P, KC, N])
        res = sb("res", [P, KC, N])
        a32 = sb("a32", [P, KN, C])
        kst = sb("kst", [P, H, C], F32R)
        qst = sb("qst", [P, H, C], F32R)
        vt = sb("vt", [P, KC, N])
        pt = sb("pt", [P, 8, 2 * C])
        rec = sb("rec", [P, C])
        pts = sb("pts", [P, 4, C])
        os_ = sb("os_", [P, 2, G, C], F32R)
        mx = sb("mx", [P, 2, H])
        mrow = sb("mrow", [H // 2, 2, C], F32R)
        st6 = sb("st6", [P, KC, 6])
        mv = sb("mv", [P, KC, 2])
        var_sum, var_mean, mean_diff2 = (sb(n, [P, KC]) for n in ("var_sum", "var_mean", "mean_diff2"))
        nmean = sb("nmean", [P, KC])
        var_eps = sb("var_eps", [P, KC])
        rstd = sb("rstd", [P, KC])

        o32 = a32
        x1T = xs[:, :, :].rearrange("p a (k t) -> p a k t", k=KN)
        aT = cs[:, :, :].rearrange("p a (k t) -> p a k t", k=KN)
        xk = xs[:, :, :].rearrange("p a (k n) -> p a k n", k=KC)
        ck = cs[:, :, :].rearrange("p a (k n) -> p a k n", k=KC)
        gpv = gp[:, :].rearrange("p (m w a c) -> p m w a c", m=KN, w=2, a=2)
        qs = gp[:, :].rearrange("p (a g t) -> p a g t", a=2, g=G)

        ST = [bank("ST0"), bank("ST1")]
        PV = bank("PV")
        CB = [bank("C0"), bank("C1")]
        DB = [bank("D0"), bank("D1")]
        EB = bank("E")
        SB = [(DB + ST)[n % 4] if n < 10 else ST[n % 2] for n in range(H)]

        vec_in = sem("vec_in", 0)
        stage_in = [sem(f"stage_in{i}", 0) for i in range(6)]
        const_done = sem("const_done", 0)
        stack_set = sem("stack_set", 0)
        ident_set = sem("ident_set", 0)
        qst_set = sem("qst_set", 0)
        mask_done = sem("mask_done", 0)
        mask_row_done = sem("mask_row_done", 0)
        setup_bn = sem("setup_bn", 0)
        setup_g = sem("setup_g", 0)
        gate_done = sem("gate_done", 0)
        w_high = sem("w_high", 0)
        w_low = sem("w_low", 0)
        wq_low = sem("wq_low", 0)
        small_high = sem("small_high", 0)
        small_low = sem("small_low", 0)
        ww_scaled = sem("ww_scaled", 0)
        wwT_full = sem("wwT_full", 0)
        wwT_done = sem("wwT_done", 0)
        bias_stored = sem("bias_stored", 0)

        HALF_IN = (2 * 5 + 1) * 16
        x_in, c_in = sem("x_in", 16), sem("c_in", 16)
        half_in = [sem(f"half{i}_in", HALF_IN) for i in range(2)]
        k_moved = [sem(f"k_moved{i}", 4) for i in range(2)]
        q_moved = [sem(f"q_moved{i}", 4) for i in range(2)]
        mrow_in, stored = sem("mrow_in", 64), sem("stored", 16)

        pg_full, th_full, aT_full = sem("pg_full", 2), sem("th_full", 1), sem("aT_full", 2)
        M_full, A_full, wy_full, x1T_full = sem("M_full", 1), sem("A_full", 1), sem("wy_full", 2), sem("x1T_full", 2)
        K_full, Q_full, V_full = sem("K_full", 2), sem("Q_full", 2), sem("V_full", 2)
        pre_full, mT_full = sem("pre_full", H), sem("mT_full", 2)
        ST_full, PV_full, O_full = sem("ST_full", H), sem("PV_full", G), sem("O_full", 2)

        pg32_done, pgH_done, pgL_done = sem("pg32_done", 2), sem("pgH_done", 2), sem("pgL_done", 2)
        thH_done, thL_done = sem("thH_done", 1), sem("thL_done", 1)
        a32_done, aH_done, aL_done = sem("a32_done", 4), sem("aH_done", 2), sem("aL_done", 2)
        m32_done, MH_done, ML_done = sem("m32_done", 2), sem("MH_done", 1), sem("ML_done", 1)
        AH_done, AL_done = sem("AH_done", 1), sem("AL_done", 1)
        x1_done, x1TH_done, x1TL_done = sem("x1_done", 2), sem("x1TH_done", 2), sem("x1TL_done", 2)
        KH_done, KL_done = sem("KH_done", 2), sem("KL_done", 2)
        QH_done, QL_done = sem("QH_done", 2), sem("QL_done", 2)
        V_done = sem("V_done", 2)
        max_done, mH_done, mL_done = sem("max_done", H), sem("mH_done", 2), sem("mL_done", 2)
        pts_done = sem("pts_done", H)
        exp_done, rec_done, o32_done = sem("exp_done", H), sem("rec_done", G), sem("o32_done", G)
        oH_done, oL_done, out_done = sem("oH_done", 2), sem("oL_done", 2), sem("out_done", 2)
        res_done = sem("res_done", 1)
        st6_done, mv_done, ve_done, rstd_done, xhat_done = (
            sem("st6_done", 2), sem("mv_done", 5), sem("ve_done", 1), sem("rstd_done", 1), sem("xhat_done", 2))
        nmean_done, centred = sem("nmean_done", 1), sem("centred", 2)
        xH_done, xL_done = sem("xH_done", 1), sem("xL_done", 1)
        cH_done, cL_done = sem("cH_done", 1), sem("cL_done", 1)

        small = x1[:, :, :].rearrange("p a b -> p (a b)")
        s_wpg = small[:, 0:512].rearrange("p (k n) -> p k n", k=KC)
        s_th = small[:, 512:768].rearrange("p (k n) -> p k n", k=KC)
        s_ww = small[:, 768:1024].rearrange("p (k n) -> p k n", k=KC)
        stage = [
            [(0, KN, pt[:, 0:4, :])],
            [(0, KN, pt[:, 4:8, :])],
            [(0, 2, res[:, :, :]), (2, KN, pts[:, :, :].rearrange("p (k a) c -> p k (a c)", k=2))],
            [(0, KN, pt[:, 0:4, :])],
        ]
        CUT = [sum(len(stage[m]) for m in range(n + 1)) for n in range(4)]
        CUT_LOW = {n: CUT[n] - (n > 0) * len(stage[1]) for n in (0, 2, 3)}
        big = [(wk, wkT), (wq, wqT), (wv, wvT), (wo, woT)]

        STN = [8 * (k // 8) + 2 * (k % 4) + (k % 8) // 4 for k in range(H)]

        block = ctx.enter_context(nc.Block())

        @block.sync
        def _(sp):
            def load_c(s):
                after_plain(sp, aT_full, s, 0)
                sp.dma_start(cin[:, :, :], ctx2[s].rearrange("(k p) n -> p k n", p=P)).then_inc(c_in[0], 16)

            def load_x(s):
                after_plain(sp, x1_done, s, 0)
                after_plain(sp, xL_done, s, 0)
                sp.dma_start(xin[:, :, :], x[s].rearrange("(k p) n -> p k n", p=P)).then_inc(x_in[0], 16)

            def low_rows(s, half, dst, low, row, done):
                after_plain(sp, done, s, half + 1)
                d = dst[:, :, :].rearrange("p (f j g) t -> p f j g t", f=2, j=4)
                for j in range(4):
                    sp.dma_start(d[row:row + DH, half, j, :, :].bitcast(F32),
                                 low[DH * j:DH * j + DH, 2 * half:2 * half + 2, :].bitcast(F32)
                                 ).then_inc(half_in[half][0], 16)

            def high_again(s, half, dst, row, moved):
                after_plain(sp, moved[half], s, 4)
                sp.dma_start(dst[row:row + DH, 8 * half:8 * half + 8, :].bitcast(F32),
                             dst[0:DH, 8 * half:8 * half + 8, :].bitcast(F32)).then_inc(half_in[half][0], 16)

            def stack_k(s, half):
                after_plain(sp, ST_full, s, 8 * half - 8)
                if is_first(s) and half == 0:
                    sp.wait_ge(bias_stored[0], 16)
                    sp.wait_ge(stack_set[0], 1)
                sp.dma_start(kst[R_MASK:R_MASK + 1, 8 * half:8 * half + 8, :].bitcast(F32),
                             mask_bias[s].rearrange("(o n) -> o n", o=1).unsqueeze(1).to_broadcast([1, 8, C])
                             ).then_inc(half_in[half][0], 16)
                low_rows(s, half, kst, ks[:, 1, :, :], 2 * DH, KL_done)

            def stack_q(s, half):
                low_rows(s, half, qst, qs[:, 1, :, :], DH, QL_done)
                high_again(s, half, qst, 2 * DH, q_moved)

            def load_weight(n):
                for k0, k1, place in stage[n]:
                    sp.dma_start(place, big[n][1][k0 * P:k1 * P, :].rearrange("(k p) n -> p k n", p=P)
                                 ).then_inc(stage_in[n][0], 16)

            load_c(0)
            sp.dma_start(small[:, 0:512], wpgT.rearrange("(k p) n -> p k n", p=P)).then_inc(stage_in[4][0], 16)
            load_x(0)
            sp.dma_start(vec[:, :], cols).then_inc(vec_in[0], 16)
            sp.dma_start(bias_pg[:, :], pgb).then_inc(vec_in[0], 16)
            sp.dma_start(mask8[:, :], mask).then_inc(vec_in[0], 16)
            sp.dma_start(s_th, thT.rearrange("(k p) n -> p k n", p=P)).then_inc(stage_in[5][0], 16)
            sp.dma_start(s_ww, ww.rearrange("(k p) n -> p k n", p=P)).then_inc(stage_in[5][0], 16)
            for n in range(3):
                load_weight(n)
            sp.wait_ge(mask_row_done[0], 1)
            sp.dma_start(mask_bias, mask_row[:, :].bitcast(F32)).then_inc(bias_stored[0], 16)
            load_c(1)
            sp.wait_ge(w_high[0], 1)
            sp.wait_ge(w_low[0], CUT_LOW[0])
            load_weight(3)

            def turn(cb, nb, pb):
                if pb is not None and cb is not None:
                    load_c(pb)
                if nb is not None:
                    stack_k(nb, 0)
                    if cb is None:
                        stack_k(nb, 1)
                    high_again(nb, 0, kst, DH, k_moved)
                    if pb is not None and cb is not None:
                        load_x(pb)
                    stack_q(nb, 0)
                    if cb is None:
                        load_x(pb)
                    else:
                        stack_k(nb, 1)
                    high_again(nb, 1, kst, DH, k_moved)
                    stack_q(nb, 1)
                    for half in range(2):
                        for a, s in enumerate((mH_done, mL_done)):
                            after_plain(sp, s, nb, half + 1)
                            sp.dma_start(qst[R_M + a:R_M + a + 1, 8 * half:8 * half + 8, :].bitcast(F32),
                                         mrow[:, a, :].bitcast(F32)).then_inc(mrow_in[0], 16)
                if cb is not None and nb is not None:
                    after_plain(sp, out_done, cb, 2)
                    sp.dma_start(out[cb].rearrange("(k p) n -> p k n", p=P), res[:, :, :]).then_inc(stored[0], 16)
                if nb is None:
                    for i in range(KC):
                        after(sp, out_done, cb, i + 1)
                        sp.dma_start(out[cb, i * P:(i + 1) * P, :], res[:, i, :]).then_inc(stored[0], 16)

            turn(None, 0, 1)
            turn(0, 1, 2)
            with sp.Fori(1, B - 2) as i:
                turn(i, i + 1, i + 2)
            turn(B - 2, B - 1, None)
            turn(B - 1, None, None)
            sp.wait_ge(stored[0], 16 * (B - 1 + KC))

        @block.gpsimd
        def _(pool):
            pool.memset(ident[:, :], 0.0).then_inc(ident_set[0], 1)
            pool.memset(ones[:, :], 1.0).then_inc(const_done[0], 1)
            pool.memset(neg_half[:, :], -0.5).then_inc(const_done[0], 1)
            pool.wait_ge(ident_set[0], 1)
            pool.affine_select(out=ident[:, :], in_=ident[:, :], compare_op=ALU.not_equal, fill=1.0,
                               base=0, pattern=[[-1, P]], channel_multiplier=1).then_inc(const_done[0], 1)

            def make_rstd(s):
                after(pool, ve_done, s, 1)
                pool.tensor_tensor(rstd[:, :], var_eps[:, :], neg_half[:, :], ALU.pow).then_inc(rstd_done[0], 1)

            def x_low(s):
                after(pool, xH_done, s, 1)
                pool.tensor_tensor(xs[:, 1, :], xin[:, :, :].rearrange("p k n -> p (k n)"),
                                   xs[:, 0, :].bitcast(F32), ALU.subtract).then_inc(xL_done[0], 1)

            def c_low(s):
                after(pool, cH_done, s, 1)
                pool.tensor_tensor(cs[:, 1, :], cin[:, :, :].rearrange("p k n -> p (k n)"),
                                   cs[:, 0, :].bitcast(F32), ALU.subtract).then_inc(cL_done[0], 1)

            pool.wait_ge(const_done[0], 3)
            pool.memset(kst[RQ:P, :, :].bitcast(F32), -1.0).then_inc(stack_set[0], 1)
            pool.wait_ge(stack_set[0], 1)
            make_rstd(0)
            x_low(0)
            pool.wait_ge(setup_bn[0], 1)
            pool.tensor_tensor(bn_tmp[:, :], bn_scale[:, :], neg_half[:, :], ALU.pow).then_inc(setup_g[0], 1)
            pool.wait_ge(setup_g[0], 1)
            pool.memset(qst[RQ:P, :, :].bitcast(F32), 1.0).then_inc(qst_set[0], 1)
            pool.wait_ge(qst_set[0], 1)

            def phi_g_low(s):
                for i in range(2):
                    after(pool, pgH_done, s, i + 1)
                    src = pg32[:, 2 * i:2 * i + 2, :].rearrange("p m (w c) -> p m w c", w=2)
                    pool.tensor_tensor(gpv[:, 2 * i:2 * i + 2, :, 1, :], src,
                                       gpv[:, 2 * i:2 * i + 2, :, 0, :].bitcast(F32),
                                       ALU.subtract).then_inc(pgL_done[0], 1)

            def cut_low(n):
                pool.wait_ge(w_high[0], CUT[n])
                w = big[n][0]
                for k0, k1, place in stage[n]:
                    pool.tensor_tensor(w[:, 1, k0:k1, :], place, w[:, 0, k0:k1, :].bitcast(F32),
                                       ALU.subtract).then_inc(w_low[0], 1)

            phi_g_low(0)

            def turn(cb, nb, pb):
                def out_low(i):
                    after(pool, oH_done, cb, i + 1)
                    pool.tensor_tensor(os_[:, 1, 2 * i:2 * i + 2, :], o32[:, 2 * i:2 * i + 2, :],
                                       os_[:, 0, 2 * i:2 * i + 2, :].bitcast(F32),
                                       ALU.subtract).then_inc(oL_done[0], 1)

                if cb is None:
                    cut_low(0)
                    cut_low(2)
                else:
                    for k in range(H if nb is not None else 0):
                        after(pool, exp_done, cb, k + 1)
                        if k % 4 == 0:
                            after(pool, PV_full, cb, k // 4)
                        pool.tensor_tensor(pts[:, k % 4, :], pt[:, k % 8, 0:C], pt[:, k % 8, C:2 * C],
                                           ALU.add).then_inc(pts_done[0], 1)
                        if k == 11:
                            out_low(0)
                    if nb is None:
                        out_low(0)
                    out_low(1)
                if pb is not None:
                    make_rstd(pb)
                    c_low(pb)
                    x_low(pb)
                    if cb is None:
                        cut_low(3)
                    phi_g_low(pb)

            turn(None, 0, 1)
            turn(0, 1, 2)
            with pool.Fori(1, B - 2) as i:
                turn(i, i + 1, i + 2)
            turn(B - 2, B - 1, None)
            turn(B - 1, None, None)

        @block.scalar
        def _(act):
            def x_high(s):
                after(act, x_in, s, 16)
                after(act, Q_full, s, 0)
                act.activation(xs[:, 0, :], xin[:, :, :].rearrange("p k n -> p (k n)"), ACT.Copy).then_inc(xH_done[0], 1)

            def c_high(s):
                after(act, c_in, s, 16)
                after(act, V_full, s, 0)
                act.activation(cs[:, 0, :], cin[:, :, :].rearrange("p k n -> p (k n)"), ACT.Copy).then_inc(cH_done[0], 1)

            def normalise(s):
                after(act, cH_done, s, 1)
                after(act, cL_done, s, 1)
                after(act, nmean_done, s, 1)
                for k in range(KC):
                    act.activation(cin[:, k, :], cin[:, k, :], ACT.Identity, bias=nmean[:, k:k + 1]
                                   ).then_inc(centred[0], 1)
                after(act, rstd_done, s, 1)
                for k in range(KC):
                    after(act, centred, s, k + 1)
                    act.activation(cin[:, k, :], cin[:, k, :], ACT.Identity, scale=rstd[:, k:k + 1]
                                   ).then_inc(xhat_done[0], 1)

            def theta_high(s):
                after(act, th_full, s, 1)
                act.activation(ths[:, 0, :], CB[0][:, :], ACT.Identity,
                               bias=vec[:, V_THB:V_THB + 1]).then_inc(thH_done[0], 1)

            def a_transposed_out(s, cb):
                after(act, aL_done, s, 0)
                if cb is not None:
                    after(act, oL_done, cb, 2)
                for d in range(KN):
                    if d % 2 == 0:
                        after(act, aT_full, s, d // 2 + 1)
                    act.activation(a32[:, d, :], DB[d // 2][:, (d % 2) * C:(d % 2) * C + C], ACT.Identity,
                                   bias=vec[:, V_LB + d:V_LB + d + 1],
                                   scale=vec[:, V_LG + d:V_LG + d + 1]).then_inc(a32_done[0], 1)
                    if d % 2:
                        after(act, a32_done, s, d + 1)
                        after(act, pg_full, s, 2)
                        act.activation(aT[:, 0, d - 1:d + 1, :], a32[:, d - 1:d + 1, :], ACT.Copy
                                       ).then_inc(aH_done[0], 1)

            def cut_high(n):
                act.wait_ge(stage_in[n][0], 16 * len(stage[n]))
                for k0, k1, place in stage[n]:
                    act.activation(big[n][0][:, 0, k0:k1, :], place, ACT.Copy).then_inc(w_high[0], 1)

            c_high(0)
            x_high(0)
            act.wait_ge(vec_in[0], 48)
            act.activation(gate_t[:, :], vec[:, V_GATE:V_GATE + 1], ACT.Tanh).then_inc(gate_done[0], 1)
            normalise(0)
            cut_high(0)
            theta_high(0)
            a_transposed_out(0, None)

            def turn(cb, nb, pb):
                TB = ST if nb is not None else ST + DB

                def exp(k):
                    if cb is None:
                        return
                    if k % 4 == 0:
                        after(act, PV_full, cb, max(k // 4 - 1, 0))
                    if k == 0 and is_first(cb):
                        act.wait_ge(w_low[0], CUT_LOW[3])
                    after(act, ST_full, cb, k + 1)
                    act.activation(pt[:, k % 8, :], TB[k % len(TB)][:, :], ACT.Exp, scale=SCALE).then_inc(exp_done[0], 1)

                def keep_x1():
                    after(act, stored, cb, 0)
                    after(act, x1_done, cb, 2)
                    act.activation(res[:, :, :], x1[:, :, :], ACT.Copy).then_inc(res_done[0], 1)

                def high(full, bank_, dst, i, done, free, free_k):
                    after(act, free, nb, free_k)
                    after(act, full, nb, i + 1)
                    act.activation(dst[:, 0, 2 * i:2 * i + 2, :], bank_[:, :].rearrange("p (a t) -> p a t", a=2),
                                   ACT.Copy).then_inc(done[0], 1)

                k_high = lambda i: high(K_full, DB[i], ks, i, KH_done, pre_full, 0)
                q_high = lambda i: high(Q_full, DB[i], qs, i, QH_done, M_full, 1)
                x1T_high = lambda i: high(x1T_full, CB[i], x1T, i, x1TH_done, th_full, 1)

                def move(dst, src, half, j, done, moved):
                    after(act, ST_full, nb, 8 * half - 8)
                    after(act, done, nb, half + 1)
                    n = 8 * half + 2 * j
                    act.activation(dst[0:DH, n:n + 2, :], src[DH * j:DH * j + DH, 0, 2 * half:2 * half + 2, :].bitcast(F32),
                                   ACT.Copy).then_inc(moved[half][0], 1)

                k_move = lambda half, j: move(kst, ks, half, j, KH_done, k_moved)
                q_move = lambda half, j: move(qst, qs, half, j, QH_done, q_moved)

                def values(i):
                    if cb is not None:
                        after(act, PV_full, cb, 4)
                    after(act, V_full, nb, i + 1)
                    act.activation(vt[:, i, :], CB[i][:, :], ACT.Copy).then_inc(V_done[0], 1)

                projects, attends = nb is not None, cb is not None
                exp(0)
                exp(1)
                if projects:
                    if cb is None:
                        cut_high(1)
                        cut_high(2)
                exp(2)
                exp(3)
                if projects:
                    k_high(0)
                if attends and projects:
                    keep_x1()
                for k in range(4, 8):
                    exp(k)
                if projects and attends:
                    k_high(1)
                if projects:
                    x1T_high(0)
                    x1T_high(1)
                if projects and not attends:
                    k_high(1)
                for k in range(8, 12):
                    exp(k)
                    if projects:
                        k_move(0, k - 8)
                if projects:
                    q_high(0)
                    q_move(0, 0)
                    q_move(0, 1)
                exp(12)
                if projects:
                    q_move(0, 2)
                    q_move(0, 3)
                exp(13)
                exp(14)
                exp(15)
                if projects:
                    q_high(1)
                    for j in range(4):
                        k_move(1, j)
                    for j in range(4):
                        q_move(1, j)
                if pb is not None and cb is None:
                    c_high(pb)
                if projects:
                    values(0)
                if pb is not None and cb is not None:
                    c_high(pb)
                if projects:
                    values(1)
                if pb is not None:
                    if cb is None:
                        cut_high(3)
                    x_high(pb)
                    normalise(pb)
                    a_transposed_out(pb, cb)
                    theta_high(pb)

            turn(None, 0, 1)
            turn(0, 1, 2)
            with act.Fori(1, B - 2) as i:
                turn(i, i + 1, i + 2)
            turn(B - 2, B - 1, None)
            turn(B - 1, None, None)

        @block.vector
        def _(dve):
            def stats(s):
                after(dve, c_in, s, 16)
                for k in range(KC):
                    dve.bn_stats(st6[:, k, :], cin[:, k, :]).then_inc(st6_done[0], 1)
                after(dve, st6_done, s, KC)
                dve.tensor_tensor(mv[:, :, 0], st6[:, :, 1], st6[:, :, 4], ALU.add).then_inc(mv_done[0], 1)
                dve.tensor_tensor(mv[:, :, 1], st6[:, :, 1], st6[:, :, 4], ALU.subtract).then_inc(mv_done[0], 1)
                dve.tensor_tensor(var_sum[:, :], st6[:, :, 2], st6[:, :, 5], ALU.add).then_inc(mv_done[0], 1)
                after(dve, mv_done, s, 3)
                dve.tensor_scalar(nmean[:, :], mv[:, :, 0], -0.5, None, ALU.mult).then_inc(nmean_done[0], 1)
                dve.tensor_scalar(var_mean[:, :], var_sum[:, :], 1.0 / N, LN_EPS, ALU.mult, ALU.add).then_inc(mv_done[0], 1)
                dve.scalar_tensor_tensor(out=mean_diff2[:, :], in0=mv[:, :, 1], scalar=0.25, in1=mv[:, :, 1],
                                         op0=ALU.mult, op1=ALU.mult).then_inc(mv_done[0], 1)
                after(dve, mv_done, s, 5)
                dve.tensor_tensor(var_eps[:, :], var_mean[:, :], mean_diff2[:, :], ALU.add).then_inc(ve_done[0], 1)

            def theta_low(s):
                after(dve, thH_done, s, 1)
                dve.scalar_tensor_tensor(out=ths[:, 1, :], in0=CB[0][:, :], scalar=vec[:, V_THB:V_THB + 1],
                                         in1=ths[:, 0, :].bitcast(F32), op0=ALU.add,
                                         op1=ALU.subtract).then_inc(thL_done[0], 1)

            def phi_g_high(s, i):
                after(dve, pgL_done, s, 0)
                after(dve, pg_full, s, i + 1)
                dve.tensor_tensor(pg32[:, 2 * i:2 * i + 2, :], CB[i][:, :].rearrange("p (m n) -> p m n", m=2),
                                  bias_pg[:, :].unsqueeze(1).to_broadcast([P, 2, 2 * CI]), ALU.add
                                  ).then_inc(pg32_done[0], 1)
                after(dve, pg32_done, s, i + 1)
                dve.tensor_copy(gpv[:, 2 * i:2 * i + 2, :, 0, :],
                                pg32[:, 2 * i:2 * i + 2, :].rearrange("p m (w c) -> p m w c", w=2)
                                ).then_inc(pgH_done[0], 1)

            def a_low(s):
                for i in range(2):
                    after(dve, aH_done, s, i + 1)
                    dve.tensor_tensor(aT[:, 1, 2 * i:2 * i + 2, :], a32[:, 2 * i:2 * i + 2, :],
                                      aT[:, 0, 2 * i:2 * i + 2, :].bitcast(F32), ALU.subtract).then_inc(aL_done[0], 1)

            stats(0)
            dve.wait_ge(stage_in[4][0], 16)
            dve.tensor_copy(wpg[:, 0, :, :], s_wpg).then_inc(small_high[0], 1)
            dve.wait_ge(small_high[0], 1)
            dve.tensor_tensor(wpg[:, 1, :, :], s_wpg, wpg[:, 0, :, :].bitcast(F32), ALU.subtract).then_inc(small_low[0], 1)
            after(dve, cH_done, 0, 1)
            dve.tensor_tensor(cs[:, 1, :], cin[:, :, :].rearrange("p k n -> p (k n)"),
                              cs[:, 0, :].bitcast(F32), ALU.subtract).then_inc(cL_done[0], 1)
            dve.wait_ge(vec_in[0], 48)
            dve.tensor_scalar(bn_scale[:, :], vec[:, V_VAR:V_VAR + KC], BN_EPS, None, ALU.add).then_inc(setup_bn[0], 1)
            dve.tensor_scalar(rec[0:B, :], mask8[:, :], 1.0, MASKED, ALU.subtract, ALU.mult).then_inc(mask_done[0], 1)
            dve.wait_ge(mask_done[0], 1)
            dve.tensor_reduce(no_key[:, :], rec[0:B, :], AX.X, ALU.max).then_inc(mask_done[0], 1)
            dve.wait_ge(mask_done[0], 2)
            dve.tensor_scalar(no_key[:, :], no_key[:, :], MASKED, None, ALU.mult).then_inc(mask_done[0], 1)
            dve.wait_ge(mask_done[0], 3)
            dve.tensor_scalar(mask_row[:, :], rec[0:B, :], no_key[:, 0:1], None, ALU.add).then_inc(mask_row_done[0], 1)
            dve.wait_ge(stage_in[5][0], 32)
            dve.tensor_copy(thw[:, 0, :, :], s_th).then_inc(small_high[0], 1)
            dve.wait_ge(small_high[0], 2)
            dve.tensor_tensor(thw[:, 1, :, :], s_th, thw[:, 0, :, :].bitcast(F32), ALU.subtract).then_inc(small_low[0], 1)
            dve.wait_ge(setup_g[0], 1)
            dve.tensor_tensor(bn_scale[:, :], bn_tmp[:, :], vec[:, V_GAM:V_GAM + KC], ALU.mult).then_inc(setup_bn[0], 1)
            dve.tensor_tensor(bn_shift[:, :], vec[:, V_WB:V_WB + KC], vec[:, V_MEAN:V_MEAN + KC],
                              ALU.subtract).then_inc(setup_bn[0], 1)
            dve.wait_ge(setup_bn[0], 3)
            dve.tensor_tensor(bn_tmp[:, :], bn_shift[:, :], bn_scale[:, :], ALU.mult).then_inc(setup_bn[0], 1)
            for k in range(KC):
                dve.tensor_scalar(s_ww[:, k, :], s_ww[:, k, :], bn_scale[:, k:k + 1], None,
                                  ALU.mult).then_inc(ww_scaled[0], 1)
            dve.wait_ge(setup_bn[0], 4)
            dve.tensor_tensor(bn_shift[:, :], bn_tmp[:, :], vec[:, V_BET:V_BET + KC], ALU.add).then_inc(setup_bn[0], 1)
            phi_g_high(0, 0)
            phi_g_high(0, 1)
            dve.wait_ge(wwT_full[0], 1)
            dve.tensor_copy(wwT[:, 0, :], EB[:, 0:C]).then_inc(wwT_done[0], 1)
            dve.wait_ge(wwT_done[0], 1)
            dve.tensor_tensor(wwT[:, 1, :], EB[:, 0:C], wwT[:, 0, :].bitcast(F32), ALU.subtract).then_inc(wwT_done[0], 1)
            theta_low(0)
            dve.wait_ge(gate_done[0], 1)

            def turn(cb, nb, pb):
                def low(done_h, bank_, dst, hi, i, s, done):
                    after(dve, done_h, s, i + 1)
                    dve.tensor_tensor(dst, bank_[:, :].rearrange("p (a t) -> p a t", a=2), hi.bitcast(F32),
                                      ALU.subtract).then_inc(done[0], 1)

                AB = [PV] if nb is not None else [PV, EB]

                def attended(g):
                    if cb is None:
                        return
                    if g == 0:
                        if nb is not None:
                            after(dve, aL_done, nb, 2)
                        after(dve, oL_done, cb, 0)
                    after(dve, PV_full, cb, g + 1)
                    if len(AB) > 1:
                        after(dve, o32_done, cb, g)
                    src = AB[g % len(AB)]
                    dve.reciprocal(rec[:, :], src[:, C:2 * C]).then_inc(rec_done[0], 1)
                    after(dve, rec_done, cb, g + 1)
                    dve.tensor_tensor(o32[:, g, :], src[:, 0:C], rec[:, :], ALU.mult).then_inc(o32_done[0], 1)
                    if g % 2:
                        i = g // 2
                        after(dve, O_full, cb, 0)
                        after(dve, o32_done, cb, g + 1)
                        dve.tensor_copy(os_[:, 0, g - 1:g + 1, :], o32[:, g - 1:g + 1, :]).then_inc(oH_done[0], 1)

                if nb is not None:
                    after(dve, M_full, nb, 1)
                    dve.tensor_scalar(m32[:, 0, :], PV[:, 0:P], 1.0 / N, None, ALU.mult).then_inc(m32_done[0], 1)
                    after(dve, m32_done, nb, 1)
                    dve.scalar_tensor_tensor(out=m32[:, 1, :], in0=PV[:, P:2 * P], scalar=1.0 / N, in1=m32[:, 0, :],
                                             op0=ALU.mult, op1=ALU.add).then_inc(m32_done[0], 1)
                    after(dve, m32_done, nb, 2)
                    dve.tensor_copy(ms[:, 0, :], m32[:, 1, :]).then_inc(MH_done[0], 1)
                    after(dve, MH_done, nb, 1)
                    dve.tensor_tensor(ms[:, 1, :], m32[:, 1, :], ms[:, 0, :].bitcast(F32),
                                      ALU.subtract).then_inc(ML_done[0], 1)
                    after(dve, A_full, nb, 1)
                    dve.tensor_copy(as_[:, 0, :], EB[:, 0:C]).then_inc(AH_done[0], 1)
                    after(dve, AH_done, nb, 1)
                    dve.tensor_tensor(as_[:, 1, :], EB[:, 0:C], as_[:, 0, :].bitcast(F32),
                                      ALU.subtract).then_inc(AL_done[0], 1)
                k_low = lambda i: low(KH_done, DB[i], ks[:, 1, 2 * i:2 * i + 2, :], ks[:, 0, 2 * i:2 * i + 2, :],
                                      i, nb, KL_done)
                q_low = lambda i: low(QH_done, DB[i], qs[:, 1, 2 * i:2 * i + 2, :], qs[:, 0, 2 * i:2 * i + 2, :],
                                      i, nb, QL_done)
                x1T_low = lambda i: low(x1TH_done, CB[i], x1T[:, 1, 2 * i:2 * i + 2, :],
                                        x1T[:, 0, 2 * i:2 * i + 2, :], i, nb, x1TL_done)

                def sum_x1():
                    if cb is not None:
                        after(dve, res_done, cb, 1)
                    for i in range(KC):
                        after(dve, wy_full, nb, i + 1)
                        dve.scalar_tensor_tensor(out=x1[:, i, :], in0=CB[i][:, :], scalar=bn_shift[:, i:i + 1],
                                                 in1=xin[:, i, :], op0=ALU.add, op1=ALU.add).then_inc(x1_done[0], 1)

                def maximum(n):
                    after(dve, pre_full, nb, n + 1)
                    dve.tensor_reduce(mx[:, :, n], SB[n][:, :].rearrange("p (a s) -> p a s", a=2),
                                      AX.X, ALU.max).then_inc(max_done[0], 1)

                def maxima_rows(half):
                    after(dve, mT_full, nb, half + 1)
                    after(dve, mrow_in, nb, 32 * half)
                    dve.tensor_copy(mrow[:, 0, :], PV[0:H // 2, 0:C]).then_inc(mH_done[0], 1)
                    after(dve, mH_done, nb, half + 1)
                    dve.tensor_tensor(mrow[:, 1, :], PV[0:H // 2, 0:C], mrow[:, 0, :].bitcast(F32),
                                      ALU.subtract).then_inc(mL_done[0], 1)

                OB = [EB, EB] if nb is not None else CB

                def final(i):
                    after(dve, O_full, cb, i + 1)
                    if nb is not None:
                        after(dve, res_done, cb, 1)
                    else:
                        after(dve, stored, cb, 0)
                    dve.scalar_tensor_tensor(out=res[:, i, :], in0=OB[i][:, :], scalar=gate_t[:, 0:1],
                                             in1=(x1 if nb is None else res)[:, i, :], op0=ALU.mult, op1=ALU.add).then_inc(out_done[0], 1)

                projects, attends = nb is not None, cb is not None
                if cb is None:
                    a_low(nb)
                    dve.wait_ge(w_high[0], CUT[1])
                    dve.tensor_tensor(wq[:, 1, :, :], stage[1][0][2], wq[:, 0, :, :].bitcast(F32),
                                      ALU.subtract).then_inc(wq_low[0], 1)
                if projects and not attends:
                    sum_x1()
                if projects:
                    k_low(0)
                if attends:
                    attended(0)
                if projects and attends:
                    sum_x1()
                if projects and attends:
                    k_low(1)
                if projects:
                    x1T_low(0)
                    x1T_low(1)
                if projects and not attends:
                    k_low(1)
                if attends:
                    attended(1)
                if projects:
                    q_low(0)
                if pb is not None:
                    stats(pb)
                if attends:
                    attended(2)
                if projects:
                    q_low(1)
                if attends:
                    attended(3)
                if projects:
                    for n in range(10):
                        maximum(n)
                if attends:
                    final(0)
                if projects:
                    maximum(10)
                    maxima_rows(0)
                    maximum(11)
                    maximum(12)
                if pb is not None:
                    phi_g_high(pb, 0)
                if projects:
                    maximum(13)
                if pb is not None:
                    phi_g_high(pb, 1)
                if projects:
                    maximum(14)
                    maximum(15)
                if projects and not attends:
                    maxima_rows(1)
                if pb is not None:
                    a_low(pb)
                if projects and attends:
                    maxima_rows(1)
                if pb is not None:
                    theta_low(pb)
                if attends:
                    final(1)

            turn(None, 0, 1)
            turn(0, 1, 2)
            with dve.Fori(1, B - 2) as i:
                turn(i, i + 1, i + 2)
            turn(B - 2, B - 1, None)
            turn(B - 1, None, None)

        @block.tensor
        def _(pe):
            PASSES = ((0, 0), (0, 1), (1, 0))

            def product(dst, depth, left, right, only=None):
                jobs = [(k, a, b) for k in range(depth) for a, b in PASSES]
                last = None
                for n, (k, a, b) in enumerate(jobs):
                    if only is None or n in only:
                        last = pe.matmul(dst, left(a, k), right(b, k), start=(n == 0), stop=(n == len(jobs) - 1))
                return last

            def a_transposed(s_, nb):
                after(pe, xhat_done, s_, 2)
                for d in range(KN):
                    if d % 2 == 0 and nb is not None:
                        after(pe, max_done, nb, 9 + d // 2)
                    for s in range(KC):
                        last = pe.transpose(DB[d // 2][:, (d % 2) * C + s * P:(d % 2) * C + (s + 1) * P],
                                            cin[:, s, d * P:(d + 1) * P], ident[:, :])
                    if d % 2:
                        last.then_inc(aT_full[0], 1)

            def phi_g(s, i, nb):
                after(pe, cH_done, s, 1)
                after(pe, cL_done, s, 1)
                if nb is not None:
                    after(pe, V_done, nb, i + 1)
                for m in (2 * i, 2 * i + 1):
                    last = product(CB[i][:, (m % 2) * 256:(m % 2) * 256 + 256], KC,
                                   lambda a, k: ck[:, a, k, m * P:(m + 1) * P], lambda b, k: wpg[:, b, k, :])
                last.then_inc(pg_full[0], 1)

            def theta(s):
                after(pe, xH_done, s, 1)
                after(pe, xL_done, s, 1)
                after(pe, pg32_done, s, 1)
                product(CB[0][:, :], KC, lambda a, k: thw[:, a, k, :], lambda b, k: xk[:, b, k, :]
                        ).then_inc(th_full[0], 1)

            pe.wait_ge(small_low[0], 1)
            phi_g(0, 0, None)
            phi_g(0, 1, None)
            pe.wait_ge(small_low[0], 2)
            theta(0)
            pe.wait_ge(const_done[0], 3)
            pe.wait_ge(ww_scaled[0], 2)
            for k in range(KC):
                last = pe.transpose(EB[:, k * P:(k + 1) * P], s_ww[:, k, :], ident[:, :])
            last.then_inc(wwT_full[0], 1)
            a_transposed(0, None)

            def turn(cb, nb, pb):
                def m_product():
                    after(pe, pgL_done, nb, 2)
                    if cb is not None:
                        after(pe, mL_done, cb, 2)
                    for m in range(KN):
                        for a in range(2):
                            last = pe.matmul(PV[:, 0:2 * P], gpv[:, m, 1, a, :],
                                             gpv[:, m, 0, :, :].rearrange("p a c -> p (a c)"),
                                             start=(m == 0 and a == 0), stop=(m == KN - 1 and a == 1))
                    last.then_inc(M_full[0], 1)

                def a_product():
                    after(pe, ML_done, nb, 1)
                    if cb is not None:
                        after(pe, out_done, cb, 0)
                    else:
                        pe.wait_ge(wwT_done[0], 2)
                    product(EB[:, 0:C], 1, lambda a, k: ms[:, a, :], lambda b, k: wwT[:, b, :]).then_inc(A_full[0], 1)

                def w_y():
                    after(pe, AL_done, nb, 1)
                    after(pe, thL_done, nb, 1)
                    for i in range(KC):
                        product(CB[i][:, :], 1, lambda a, k: as_[:, a, i * P:(i + 1) * P],
                                lambda b, k: ths[:, b, :]).then_inc(wy_full[0], 1)

                def x1_transposed():
                    after(pe, x1_done, nb, 2)
                    for d in range(KN):
                        for s in range(KC):
                            last = pe.transpose(CB[d // 2][:, (d % 2) * C + s * P:(d % 2) * C + (s + 1) * P],
                                                x1[:, s, d * P:(d + 1) * P], ident[:, :])
                        if d % 2:
                            last.then_inc(x1T_full[0], 1)

                def k_tile(g):
                    if g == 0:
                        if is_first(nb):
                            pe.wait_ge(w_low[0], CUT_LOW[0])
                        after(pe, aL_done, nb, 2)
                    last = product(DB[g // 2][:, (g % 2) * C:(g % 2) * C + C], KN,
                                   lambda a, k: wk[:, a, k, g * P:(g + 1) * P], lambda b, k: aT[:, b, k, :])
                    if g % 2:
                        last.then_inc(K_full[0], 1)

                def q_tile(g):
                    if g == 0:
                        if is_first(nb):
                            pe.wait_ge(wq_low[0], 1)
                        after(pe, x1TL_done, nb, 2)
                    if g % 2 == 0:
                        after(pe, KL_done, nb, g // 2 + 1)
                    last = product(DB[g // 2][:, (g % 2) * C:(g % 2) * C + C], KN,
                                   lambda a, k: wq[:, a, k, g * P:(g + 1) * P], lambda b, k: x1T[:, b, k, :])
                    if g % 2:
                        last.then_inc(Q_full[0], 1)

                def scores(n):
                    if n == 0:
                        if is_first(nb):
                            pe.wait_ge(qst_set[0], 1)
                    if n % 8 == 0:
                        after(pe, half_in[n // 8], nb, HALF_IN)
                    if n < 2:
                        after(pe, QL_done, nb, n + 1)
                    elif n >= 4:
                        after(pe, max_done, nb, n - 3 if n < 12 else n - 1)
                    elif cb is not None:
                        after(pe, exp_done, cb, 13 + n)
                    for t in range(2):
                        last = pe.matmul(SB[n][:, t * C:(t + 1) * C], qst[0:R_MASK + 1, n, t * P:(t + 1) * P],
                                         kst[0:R_MASK + 1, n, :], start=True, stop=True)
                    last.then_inc(pre_full[0], 1)

                def maxima_transposed(half):
                    after(pe, max_done, nb, 8 * half + 8)
                    if half == 1:
                        after(pe, mL_done, nb, 1)
                    elif cb is not None:
                        after(pe, o32_done, cb, G)
                    else:
                        after(pe, m32_done, nb, 2)
                    for t in range(2):
                        last = pe.transpose(PV[0:H // 2, t * P:(t + 1) * P], mx[:, t, 8 * half:8 * half + 8], ident[:, :])
                    last.then_inc(mT_full[0], 1)

                TB = ST if nb is not None else ST + DB
                AB = [PV] if nb is not None else [PV, EB]
                ATTEND_AT = [5, 9, 13] if nb is not None else [7, 11, 15]

                def scores_t(k):
                    if cb is None:
                        return
                    if k % 8 == 0:
                        after(pe, mrow_in, cb, 32 * (k // 8 + 1))
                    if k < 2:
                        after(pe, max_done, cb, 15 + k)
                    elif k >= len(TB):
                        after(pe, exp_done, cb, k - len(TB) + 1)
                    n = STN[k]
                    for s in range(2):
                        last = pe.matmul(TB[k % len(TB)][:, s * C:(s + 1) * C], kst[0:R_ALL, n, s * P:(s + 1) * P],
                                         qst[0:R_ALL, n, :], start=True, stop=True)
                    last.then_inc(ST_full[0], 1)

                def attend(g):
                    if cb is None:
                        return
                    if g == 0:
                        after(pe, V_done, cb, 2)
                        after(pe, mL_done, cb, 2)
                        if nb is not None:
                            after(pe, m32_done, nb, 2)
                    after(pe, exp_done, cb, 4 * g + 4)
                    if g >= len(AB):
                        after(pe, o32_done, cb, g - len(AB) + 1)
                    elif g == 1:
                        after(pe, out_done, cb, 0)
                    dst = AB[g % len(AB)]
                    for s in range(2):
                        for j in range(4):
                            h = 4 * g + j
                            pe.matmul(dst[DH * j:DH * j + DH, 0:C], vt[:, s, DH * h:DH * h + DH],
                                      pt[:, (g % 2) * 4 + j, s * C:(s + 1) * C], start=(s == 0), stop=(s == 1))
                    if nb is None:
                        for s in range(2):
                            for j in range(4):
                                last = pe.matmul(dst[DH * j:DH * j + DH, C:2 * C], ones[:, :],
                                                 pt[:, (g % 2) * 4 + j, s * C:(s + 1) * C], start=(s == 0), stop=(s == 1))
                    else:
                        after(pe, pts_done, cb, 4 * g + 4)
                        for j in range(4):
                            last = pe.matmul(dst[DH * j:DH * j + DH, C:2 * C], ones[:, :], pts[:, j, :],
                                             start=True, stop=True)
                    last.then_inc(PV_full[0], 1)

                def v_matmuls(lo, hi):
                    for q in range(lo, hi):
                        i, w = divmod(q, 12)
                        last = product(CB[i][:, :], KN, lambda a, k: aT[:, a, k, i * P:(i + 1) * P],
                                       lambda b, k: wv[:, b, k, :], only=(w,))
                        if w == 11:
                            last.then_inc(V_full[0], 1)

                def o_matmuls(lo, hi):
                    for q in range(lo, hi):
                        i, w = divmod(q, 12)
                        if w == 0:
                            if is_first(cb):
                                pe.wait_ge(w_low[0], CUT_LOW[3])
                            if nb is not None and i == 0:
                                after(pe, AL_done, nb, 1)
                            elif nb is not None:
                                after(pe, out_done, cb, 1)
                        if w % 6 == 0:
                            after(pe, oL_done, cb, w // 6 + 1)
                        last = product((CB[i] if nb is None else EB)[:, :], KN, lambda a, k: os_[:, a, k, i * P:(i + 1) * P],
                                       lambda b, k: wo[:, b, k, :], only=(w,))
                        if w == 11:
                            last.then_inc(O_full[0], 1)

                projects, attends = nb is not None, cb is not None
                for k in range(H):
                    scores_t(k)
                    if attends and k in ATTEND_AT:
                        attend(ATTEND_AT.index(k))
                    if projects and attends:
                        if k == 1:
                            m_product()
                            k_tile(0)
                        if k == 3:
                            a_product()
                            k_tile(1)
                        if k == 5:
                            w_y()
                        if k in (6, 7):
                            k_tile(k - 4)
                        if k == 8:
                            x1_transposed()
                        if k in (10, 11, 12):
                            q_tile(k - 10)
                        if k == 14:
                            q_tile(3)
                if not attends:
                    m_product()
                    a_product()
                    w_y()
                    k_tile(0)
                    k_tile(1)
                    x1_transposed()
                    k_tile(2)
                    k_tile(3)
                    for g in range(G):
                        q_tile(g)
                if projects:
                    if is_first(nb):
                        pe.wait_ge(w_low[0], CUT_LOW[2])
                    v_matmuls(0, 4 if attends else 24)
                if attends and projects:
                    attend(G - 1)
                V_AT = {0: (4, 6), 1: (6, 10), 2: (10, 13), 3: (13, 17), 4: (17, 19), 5: (19, 21), 6: (21, 24)}
                for n in range(H if projects else 0):
                    scores(n)
                    if attends and n in V_AT:
                        v_matmuls(*V_AT[n])
                    if n == 10:
                        maxima_transposed(0)
                    if attends and 6 <= n < 10:
                        o_matmuls(3 * n - 18, 3 * n - 15)
                    if pb is None and 11 <= n < 15:
                        o_matmuls(3 * n - 21, 3 * n - 18)
                    if pb is not None and n in (11, 12):
                        phi_g(pb, n - 11, nb)
                    if pb is not None and n == 13:
                        a_transposed(pb, nb)
                    if pb is not None and n == 14:
                        theta(pb)
                if pb is not None and attends:
                    o_matmuls(12, 18)
                if projects:
                    maxima_transposed(1)
                if pb is not None and attends:
                    o_matmuls(18, 24)
                if not projects:
                    attend(G - 1)
                    for half in range(2):
                        for i in range(KC):
                            o_matmuls(12 * i + 6 * half, 12 * i + 6 * half + 6)

            turn(None, 0, 1)
            turn(0, 1, 2)
            with pe.Fori(1, B - 2) as i:
                turn(i, i + 1, i + 2)
            turn(B - 2, B - 1, None)
            turn(B - 1, None, None)


def kernel(**inputs):
    import numpy as np
    import concourse.bacc as bacc
    from concourse.bass_utils import run_bass_kernel_spmd

    a = {k: np.asarray(v) for k, v in inputs.items()}

    def by_partition(name):
        return a[name].reshape(-1, 128).T

    cols = np.concatenate([by_partition(n) for n in (
        "L0_xattn_theta_b", "L0_xattn_bn_gamma", "L0_xattn_bn_beta", "L0_xattn_bn_mean", "L0_xattn_bn_var",
        "L0_xattn_w_b", "L1_xattn_ln_gamma", "L1_xattn_ln_beta")]
        + [np.broadcast_to(a["L1_xattn_gate"].reshape(1, 1), (128, 1))], axis=1)
    arrays = {
        "x": a["x"],
        "ctx2": a["ctx_2048"],
        "mask": a["mask_BxS2_bf1"].view(np.uint8),
        "wpgT": np.concatenate([a["L0_xattn_phi_w"].T, a["L0_xattn_g_w"].T], axis=1),
        "thT": a["L0_xattn_theta_w"].T,
        "ww": a["L0_xattn_w_w"],
        "cols": cols,
        "pgb": np.broadcast_to(np.concatenate([a["L0_xattn_phi_b"], a["L0_xattn_g_b"]])[None, :], (128, 256)),
        "wkT": a["L1_xattn_Wk"].T,
        "wqT": a["L1_xattn_Wq"].T,
        "wvT": a["L1_xattn_Wv"].T,
        "woT": a["L1_xattn_Wo"].T,
    }
    arrays = {k: np.ascontiguousarray(v) for k, v in arrays.items()}
    nc = bacc.Bacc("TRN2", target_bir_lowering=False, num_devices=1)
    args = [nc.dram_tensor(k, v.shape, mybir.dt.from_np(v.dtype), kind="ExternalInput").ap()
            for k, v in arrays.items()]
    B, C, N = a["x"].shape
    args.append(nc.dram_tensor("mask_bias", (B, C), F32, kind="Internal").ap())
    args.append(nc.dram_tensor("out", (B, C, N), F32, kind="ExternalOutput").ap())
    two_layer_cross_attention(nc, *args)
    r = run_bass_kernel_spmd(nc, [arrays], core_ids=[0])
    return r.results[0]["out"]
```
